# Optimizing a Trainium2 kernel written in Bass

```python
import numpy as np
import jax
import jax.numpy as jnp

def _softmax(x, axis=-1):
    return jax.nn.softmax(x, axis=axis)

def _gelu(x):
    return jax.nn.gelu(x, approximate=True)

def _silu(x):
    return jax.nn.silu(x)

def _sigmoid(x):
    return jax.nn.sigmoid(x)

def _layernorm(x, axis=-1, eps=1e-05):
    m = jnp.mean(x, axis=axis, keepdims=True)
    v = jnp.var(x, axis=axis, keepdims=True)
    return (x - m) / jnp.sqrt(v + eps)

def _scatter_add(tgt, idx, src, axis=0):
    return tgt.at[idx].add(src)

def _segment_sum(src, seg, n):
    return jax.ops.segment_sum(src, seg, n)
kernel_name = 'mk_gnn_preln_d1_gnn_r8_11b4d7'

def setup_inputs(seed: int=0):
    np.random.seed(seed)
    _w = jnp.asarray

    def _rec_inputs():
        import jax
        import jax.numpy as jnp
        _gk = jax.random.key(seed)
        x = -0.0003713 + 1 * jax.random.normal(jax.random.fold_in(_gk, 1), (12500, 128), jnp.float32)
        src = jax.random.randint(jax.random.fold_in(_gk, 2), (200000,), 0, 12500, jnp.int32)
        dst = jax.random.randint(jax.random.fold_in(_gk, 3), (200000,), 0, 12500, jnp.int32)
        _o = jnp.argsort(dst, stable=True)
        src = src[_o]
        dst = dst[_o]
        return (x, src, dst)
    x, src, dst = _rec_inputs()

    def _L0_gnn_setup():
        import jax, jax.numpy as jnp
        import numpy as np
        N_NODES, N_EDGES, D_FEAT = (12500, 62500, 128)
        key = jax.random.key(seed)
        k1, k2, k3, k4 = jax.random.split(key, 4)
        feat = jax.random.normal(k1, (N_NODES, D_FEAT), dtype=jnp.float32)
        W = jax.random.normal(k2, (D_FEAT, 2 * D_FEAT), dtype=jnp.float32) * 0.05
        b = jnp.zeros((D_FEAT,), dtype=jnp.float32)
        src = jax.random.randint(k3, (N_EDGES,), 0, N_NODES)
        dst = jax.random.randint(k4, (N_EDGES,), 0, N_NODES)
        return {'feat': feat, 'W': W, 'b': b, 'src': src, 'dst': dst}
    _L0_gnn_all = _L0_gnn_setup()
    _L0_gnn_in = {k: v for k, v in _L0_gnn_all.items() if k in ('W', 'b')}
    del _L0_gnn_all
    return {'x': x, 'src': src, 'dst': dst, 'L0_gnn_W': _L0_gnn_in['W'], 'L0_gnn_b': _L0_gnn_in['b']}

def reference(x, src, dst, L0_gnn_W, L0_gnn_b):
    import jax
    import jax.numpy as jnp

    def _L0_gnn_ref(feat, W, b, src, dst):
        import jax, jax.numpy as jnp
        import numpy as np
        N_NODES, N_EDGES, D_FEAT = (12500, 62500, 128)
        N = feat.shape[0]
        degs = jax.ops.segment_sum(jnp.ones(dst.shape, dtype=feat.dtype), dst, num_segments=N)
        norm = jnp.maximum(degs, 1.0) ** (-0.5)
        edge_in = jnp.concatenate([feat[dst], feat[src]], axis=-1)
        msg = edge_in @ W.T + b
        msg = (norm[src] * norm[dst])[:, None] * msg
        return jax.ops.segment_sum(msg, dst, num_segments=N)
    h = jnp.maximum(_layernorm(x, axis=-1), 0.0)
    x = x + _L0_gnn_ref(h, L0_gnn_W, L0_gnn_b, src, dst)
    return x

_drawn_inputs = setup_inputs


def setup_inputs(seed=0):
    import zlib

    import numpy as np

    out = dict(_drawn_inputs(seed))
    spreads = {'L0_gnn_b': (0.0, 0.1)}
    factors = {}
    for name, (base, spread) in spreads.items():
        noise = np.random.default_rng([zlib.crc32(name.encode()), seed]).standard_normal(out[name].shape)
        drawn = base * np.exp(spread * noise) if base else spread * noise
        out[name] = jnp.asarray(drawn.astype(out[name].dtype))
    for name, factor in factors.items():
        out[name] = (out[name] * factor).astype(out[name].dtype)
    return out
```

```python
import concourse.bass as bass
from concourse import mybir
from contextlib import ExitStack


def gnn_layer(nc, x, src, dst, W, b, out):
    f32, bf16, i32 = mybir.dt.float32, mybir.dt.bfloat16, mybir.dt.int32
    ALU = mybir.AluOpType
    ACT = mybir.ActivationFunctionType
    AX = mybir.AxisListType

    N, D = x.shape
    E = src.shape[0]
    P = 128
    TILES = -(-N // P)
    LAST_ROWS = N - (TILES - 1) * P
    SPC = 16
    STEP_E = SPC * P
    STEPS = -(-E // STEP_E)
    CH = STEPS * SPC
    REAL_CH = -(-E // P)
    LAST_CH = REAL_CH - (STEPS - 1) * SPC
    FULL_ROWS = E // STEP_E
    LIST_LOADS = 48 if FULL_ROWS >= 16 else 32
    TAIL_E = E - FULL_ROWS * STEP_E
    NPC = N * P // E
    GC = 8
    GROUPS = CH // GC
    WIN = P
    BACK = (WIN - NPC) // 2
    GW = WIN + NPC * (GC - 1)
    PAD = P // 2
    COLS = TILES * P + 2 * PAD
    ROW = D + 4
    EPS = 1e-5
    FAR = -32768.0
    BATCHES = 7
    BT = TILES // BATCHES
    DB, DA = 16, 12
    CB = 4
    PASSES = 7
    PC = CH // PASSES
    PW = (PC // GC - 1) * 4 + DA
    Q = COLS // DB
    QB = TILES * P // (PASSES * DB)
    assert D == P and NPC == 8 and STEPS == TILES and TILES == BATCHES * BT and CH == PASSES * PC
    assert TILES * P == PASSES * QB * DB and E % P == P // 2
    assert PAD + TILES * P <= COLS and (GROUPS - 1) * NPC * GC + PAD - BACK + GW <= COLS

    row_of = lambda a, t, k: a[t * P:(t + k) * P, :].rearrange("(t p) d -> p t d", p=P)

    table = nc.dram_tensor("table", (TILES * P, ROW), f32, kind="Internal").ap()
    degrees = nc.dram_tensor("degrees", (TILES * P,), f32, kind="Internal").ap()

    ctx = ExitStack()
    with ctx:
        sb = lambda name, shape, dt: ctx.enter_context(nc.sbuf_tensor(name, shape, dt))
        sem = lambda name: ctx.enter_context(nc.semaphore(name))
        banks = [ctx.enter_context(nc.psum_tensor(f"bank{i}", [P, 512], f32)) for i in range(8)]

        AG = sb("AG", [P, COLS], f32)
        SR = sb("SR", [P, COLS], f32)
        HT = sb("HT", [P, TILES * ROW], f32)
        xall = AG[:, 0:TILES * P].rearrange("p (t d) -> p t d", d=D)
        H = HT[:, :].rearrange("p (t r) -> p t r", r=ROW)
        SP_ROW = 96
        raw0 = TILES * ROW - 4 * STEP_E
        dst_raw, dst_f, src_raw, src_f = (HT[0:STEPS, raw0 + i * STEP_E:raw0 + (i + 1) * STEP_E] for i in range(4))
        dst_raw, src_raw = dst_raw.bitcast(i32), src_raw.bitcast(i32)
        rel = sb("rel", [P, CH], f32)
        srci = sb("srci", [P, CH], i32)
        first = sb("first", [P, CH], i32)
        j8 = sb("j8", [P, GC], i32)
        nodes = sb("nodes", [P, WIN], f32)
        nodes_i = sb("nodes_i", [P, WIN], i32)
        ident = sb("ident", [P, P], f32)
        w_in = sb("w_in", [P, 2 * D], f32)
        wT = sb("wT", [P, 2 * D], f32)
        brow = sb("brow", [1, D + 1], f32)
        stats = sb("stats", [P, TILES, 6], f32)
        mean2 = sb("mean2", [P, TILES], f32)
        dif = sb("dif", [P, TILES], f32)
        var = sb("var", [P, TILES], f32)
        std = sb("std", [P, TILES], f32)
        rstd = sb("rstd", [P, TILES], f32)
        nmr = sb("nmr", [P, TILES], f32)
        hi_lo = sb("hi_lo", [P, 2], f32)
        worst = sb("worst", [P, 1], f32)
        flag = sb("flag", [1, 2], f32)
        flag_i = sb("flag_i", [1, 1], i32)
        mask_i = sb("mask_i", [64, 8], i32)
        lane_i = sb("lane_i", [64, DB], i32)
        lane_b = sb("lane_b", [64, 8], i32)
        diag = sb("diag", [64, CB], f32)
        pick = sb("pick", [64, DB], f32)
        cnt = sb("cnt", [64, Q], f32)
        cut = sb("cut", [64, PW * CB], f32)
        part = sb("part", [64, PW], f32)
        deg_sb = sb("deg_sb", [P, P], f32)
        deg_t = sb("deg_t", [TILES, P], f32)
        root_t = sb("root_t", [TILES, P], f32)
        norm_t = sb("norm_t", [TILES, P], f32)
        norm = sb("norm", [P, TILES], f32)
        idx = sb("idx", [P, SPC], i32)
        G = sb("G", [P, SPC, ROW], f32)
        OH = sb("OH", [P, SPC, WIN], f32)
        h_st = sb("h_st", [P, ROW], f32)
        x_st = sb("x_st", [P, D], f32)
        a_st = sb("a_st", [P, P], f32)
        s_st = sb("s_st", [1, P], f32)
        hT = sb("hT", [P, P], f32)
        t1 = sb("t1", [P, D], f32)
        o_st = sb("o_st", [P, D], f32)
        grel = sb("grel", [P, GC], f32)

        scr = SR[:, :]
        n_i, lo_i, hi_i = (scr[:, i * CH:(i + 1) * CH].bitcast(i32) for i in range(3))
        digit_b = scr[:, 3 * CH:3 * CH + CH // 2].bitcast(bf16)
        digit_a = scr[:, 3 * CH + CH // 2:4 * CH].bitcast(bf16)
        o0 = 4 * CH
        hot_b = scr[:, o0:o0 + DB * PC // 2].bitcast(bf16).rearrange("p (m v c) -> p m v c", m=PC // CB, c=CB)
        hot_a = scr[:, o0 + DB * PC // 2:o0 + (DB + DA) * PC // 2].bitcast(bf16).rearrange("p (m v c) -> p m v c", m=PC // CB, c=CB)
        lo_f, hi_f = scr[:, o0:o0 + CH], scr[:, o0 + CH:o0 + 2 * CH]
        o1 = o0 + 2 * CH
        hot_lo = scr[:, o1:o1 + GC * P // 2].bitcast(bf16).rearrange("p (j n) -> p j n", j=GC)
        hot_hi = scr[:, o1 + GC * P // 2:o1 + GC * P].bitcast(bf16).rearrange("p (j n) -> p j n", j=GC)

        dst_in = sem("dst_in")
        src_in = sem("src_in")
        x_in = [sem(f"x_in{i}") for i in range(BATCHES)]
        w_loaded = sem("w_loaded")
        edge_pads = sem("edge_pads")
        consts = sem("consts")
        pool_step = sem("pool_step")
        dve_step = sem("dve_step")
        act_step = sem("act_step")
        dst_float = sem("dst_float")
        src_float = sem("src_float")
        w_turned = sem("w_turned")
        w_ready = sem("w_ready")
        dst_turned = sem("dst_turned")
        src_turned = sem("src_turned")
        src_ready = sem("src_ready")
        worst_ready = sem("worst_ready")
        worst_turned = sem("worst_turned")
        flag_ready = sem("flag_ready")
        hot_ready = sem("hot_ready")
        counted = sem("counted")
        cnt_added = sem("cnt_added")
        norm_ready = sem("norm_ready")
        grel_ready = sem("grel_ready")
        all_hot = sem("all_hot")
        all_summed = sem("all_summed")
        all_added = sem("all_added")
        all_counted = sem("all_counted")
        all_hot_ready = sem("all_hot_ready")
        dve_step_quick = sem("dve_step_quick")
        dve_step_general = sem("dve_step_general")
        cnt_turned = sem("cnt_turned")
        deg_ready = sem("deg_ready")
        deg_in_dram = sem("deg_in_dram")
        deg_back = sem("deg_back")
        root_ready = sem("root_ready")
        deg_clamped = sem("deg_clamped")
        norm_rows = sem("norm_rows")
        norm_turned = sem("norm_turned")
        var_ready = sem("var_ready")
        std_ready = sem("std_ready")
        ln_ready = sem("ln_ready")
        h_ready = sem("h_ready")
        rows_ready = sem("rows_ready")
        table_done = sem("table_done")
        sums_clear = sem("sums_clear")
        idx_ready = sem("idx_ready")
        waited = sem("waited")
        landed = [sem(f"landed{i}") for i in range(SPC)]
        hot = sem("hot")
        chunk_used = sem("chunk_used")
        group_added = sem("group_added")
        h_loaded = sem("h_loaded")
        x_loaded = sem("x_loaded")
        h_turned = sem("h_turned")
        hT_ready = sem("hT_ready")
        staged = sem("staged")
        fin_mm = sem("fin_mm")
        t1_done = sem("t1_done")
        out_ready = sem("out_ready")
        stored = sem("stored")

        AGG_A, AGG_B, S_A, S_B, TURN, SELF, FIN = banks[0:7]
        agg_ps, s_ps = [AGG_A, AGG_B], [S_A, S_B]

        def wait_prior(eng, what, value):
            if not (isinstance(value, int) and value == 0):
                eng.wait_ge(what, value)

        def rows_of(t):
            return LAST_ROWS if isinstance(t, int) and t == TILES - 1 else P

        def flag_value(eng):
            eng.wait_ge(flag_ready, 1)
            return eng.value_load(flag_i[0:1, 0:1], min_val=0, max_val=1)

        block = ctx.enter_context(nc.Block())

        @block.sync
        def _(sp):
            sp.wait_ge(edge_pads, 2)
            for raw, lst, list_in in ((dst_raw, dst, dst_in), (src_raw, src, src_in)):
                k = FULL_ROWS // 16 * 16
                if k:
                    sp.dma_start(raw[0:k, :], lst[0:k * STEP_E].rearrange("(s e) -> s e", e=STEP_E)).then_inc(list_in, 16)
                sp.dma_start(raw[k:FULL_ROWS, :], lst[k * STEP_E:FULL_ROWS * STEP_E].rearrange("(s e) -> s e", e=STEP_E)).then_inc(list_in, 16)
                sp.dma_start(raw[FULL_ROWS:STEPS, 0:TAIL_E], lst[FULL_ROWS * STEP_E:E].rearrange("(s e) -> s e", s=1)).then_inc(list_in, 16)
            sp.dma_start(w_in[:, :], W).then_inc(w_loaded, 16)
            sp.dma_start(brow[0:1, 0:D], b.rearrange("(a d) -> a d", a=1)).then_inc(w_loaded, 16)
            for i in range(BATCHES):
                k = BT - (i == BATCHES - 1)
                sp.dma_start(xall[:, i * BT:i * BT + k, :], row_of(x, i * BT, k)).then_inc(x_in[i], 16)
            sp.wait_ge(consts, 1)
            sp.dma_start(xall[0:LAST_ROWS, TILES - 1, :], x[(TILES - 1) * P:N, :]).then_inc(x_in[BATCHES - 1], 16)

            quick = flag_value(sp)
            sp.wait_ge(deg_ready, 1)
            with sp.If(quick == 1):
                sp.dma_start(degrees.rearrange("(k q b) -> q k b", q=QB, b=DB),
                             deg_sb[0:QB, 0:PASSES * DB].rearrange("q (k b) -> q k b", b=DB)).then_inc(deg_in_dram, 16)
            with sp.Else():
                sp.dma_start(degrees.rearrange("(t n) -> t n", n=P), deg_sb[0:TILES, :]).then_inc(deg_in_dram, 16)
            sp.wait_ge(deg_in_dram, 16)
            sp.dma_start(deg_t[:, :], degrees.rearrange("(t n) -> t n", n=P)).then_inc(deg_back, 16)

            for i in range(BATCHES):
                sp.wait_ge(rows_ready, i + 1)
                sp.dma_start(row_of(table, i * BT, BT), H[:, i * BT:(i + 1) * BT, :]).then_inc(table_done, 16)
            sp.wait_ge(table_done, 16 * BATCHES)

            def load_rows(t):
                r = rows_of(t)
                wait_prior(sp, h_turned, t)
                sp.dma_start(h_st[0:r, :], table[bass.ds(t * P, r), :]).then_inc(h_loaded, 16)
                wait_prior(sp, t1_done, t)
                sp.dma_start(x_st[0:r, :], x[bass.ds(t * P, r), :]).then_inc(x_loaded, 16)

            def store_rows(t):
                r = rows_of(t)
                sp.wait_ge(out_ready, t + 1)
                sp.dma_start(out[bass.ds(t * P, r), :], o_st[0:r, :]).then_inc(stored, 16)

            load_rows(0)
            with sp.Fori(0, TILES - 2) as t:
                load_rows(t + 1)
                store_rows(t)
            load_rows(TILES - 1)
            store_rows(TILES - 2)
            store_rows(TILES - 1)
            sp.wait_ge(stored, 16 * TILES)

        @block.gpsimd
        def _(pool):
            tail = slice(FULL_ROWS // 32 * 32, STEPS)
            pool.memset(dst_raw[tail, :], N - 1).then_inc(edge_pads, 1)
            pool.wait_ge(edge_pads, 1)
            pool.memset(src_raw[tail, :], 0).then_inc(edge_pads, 1)
            pool.wait_ge(edge_pads, 2)
            pool.memset(xall[:, TILES - 1, :], 0.0).then_inc(consts, 1)
            pool.memset(ident[:, :], 0.0).then_inc(pool_step, 1)
            pool.wait_ge(pool_step, 1)
            pool.affine_select(out=ident[:, :], in_=ident[:, :], compare_op=ALU.not_equal, fill=1.0, base=0,
                               pattern=[[-1, P]], channel_multiplier=1).then_inc(consts, 1)
            pool.iota(first[:, :], pattern=[[NPC, CH]], base=-BACK, channel_multiplier=0).then_inc(consts, 1)
            pool.iota(j8[:, :], pattern=[[NPC, GC]], base=PAD - BACK, channel_multiplier=0).then_inc(consts, 1)
            pool.iota(nodes_i[:, :], pattern=[[1, WIN]], base=0, channel_multiplier=0).then_inc(consts, 1)
            pool.wait_ge(consts, 5)
            pool.iota(mask_i[:, :], pattern=[[0, 8]], base=0, channel_multiplier=1).then_inc(consts, 1)
            pool.wait_ge(consts, 6)
            pool.memset(brow[0:1, D:D + 1], 1.0).then_inc(consts, 1)
            pool.wait_ge(consts, 7)

            pool.wait_ge(h_ready, BATCHES)
            pool.memset(AG[:, :], 0.0).then_inc(sums_clear, 1)
            pool.wait_ge(sums_clear, 1)
            pool.wait_ge(deg_ready, 1)
            pool.memset(SR[SP_ROW:SP_ROW + 1, :], 0.0).then_inc(sums_clear, 1)

            quick = flag_value(pool)
            pool.wait_ge(table_done, 16 * BATCHES)

            def gather(j):
                pool.indirect_dma_start(G[:, j, :], None, table[:, :],
                                        bass.IndirectOffsetOnAxis(ap=idx[:, j:j + 1], axis=0)).then_inc(landed[j], 16)

            with pool.If(quick == 1):
                def step(i, k, prior):
                    for j in range(k):
                        if j % GC == 0:
                            pool.wait_ge(idx_ready, 2 * i + j // GC + 1)
                            pool.sem_inc(waited)
                        if prior and j % 4 == 0:
                            pool.wait_ge(chunk_used, (i - 1) * SPC + j + 4)
                            pool.sem_inc(waited)
                        gather(j)

                step(0, SPC, False)
                with pool.Fori(1, STEPS - 1) as i:
                    step(i, SPC, True)
                step(STEPS - 1, LAST_CH, True)
            with pool.Else():
                with pool.Fori(0, GROUPS) as g:
                    pool.wait_ge(idx_ready, g + 1)
                    pool.wait_ge(all_summed, g * TILES + 1)
                    pool.sem_inc(waited)
                    for j in range(GC):
                        gather(j)

        @block.scalar
        def _(act):
            act.wait_ge(src_in, LIST_LOADS)
            nc.scalar.copy(src_f, src_raw).then_inc(src_float, 1)
            act.wait_ge(w_turned, 1)
            nc.scalar.copy(wT[:, :], banks[4][:, 0:2 * D]).then_inc(w_ready, 1)
            for k in range(4):
                act.wait_ge(src_turned, k + 1)
                last = nc.scalar.copy(
                    srci[:, :].rearrange("p (s j) -> p j s", j=SPC)[:, 4 * k:4 * k + 4, :],
                    banks[4 + k][:, 0:4 * STEPS].rearrange("p (j s) -> p j s", j=4))
            last.then_inc(src_ready, 1)

            for i in range(BATCHES):
                s = slice(i * BT, (i + 1) * BT)
                act.wait_ge(var_ready, i + 1)
                nc.scalar.activation(std[:, s], var[:, s], ACT.Sqrt).then_inc(std_ready, 1)
                act.wait_ge(ln_ready, i + 1)
                if i == 2:
                    act.wait_ge(src_turned, 4)
                    act.wait_ge(dst_turned, 4)
                for t in range(i * BT, (i + 1) * BT):
                    last = nc.scalar.activation(H[:, t, 0:D], xall[:, t, :], ACT.Relu,
                                                scale=rstd[:, t:t + 1], bias=nmr[:, t:t + 1])
                last.then_inc(h_ready, 1)
            act.wait_ge(deg_clamped, 1)
            nc.scalar.activation(root_t[:, :], deg_t[:, :], ACT.Sqrt).then_inc(root_ready, 1)

            quick = flag_value(act)
            act.wait_ge(src_ready, 1)

            def hand_idx(i, half):
                nc.scalar.copy(idx[:, half * GC:(half + 1) * GC],
                               srci[:, bass.ds(i * SPC + half * GC, GC)]).then_inc(idx_ready, 1)

            def turned_h(t):
                r = rows_of(t)
                act.wait_ge(h_turned, t + 1)
                nc.scalar.copy(hT[:, 0:r], TURN[:, 0:r]).then_inc(hT_ready, 1)

            def stage(t, adds, added=group_added):
                act.wait_ge(added, adds)
                wait_prior(act, fin_mm, t)
                nc.scalar.copy(a_st[:, :], AG[:, bass.ds(t * P + PAD, P)])
                nc.scalar.copy(s_st[:, :], SR[SP_ROW:SP_ROW + 1, bass.ds(t * P + PAD, P)]).then_inc(staged, 1)

            with act.If(quick == 1):
                def step(i, ahead, t_turn, t_stage, second_ahead=True):
                    if t_turn:
                        turned_h(i - 2)
                    if ahead:
                        act.wait_ge(chunk_used, i * SPC + GC)
                        hand_idx(i + 1, 0)
                    if t_stage:
                        stage(i - 1, 2 * i + 1)
                    if ahead:
                        act.wait_ge(chunk_used, (i + 1) * SPC)
                        hand_idx(i + 1, 1)

                hand_idx(0, 0)
                hand_idx(0, 1)
                step(0, True, False, False)
                step(1, True, False, True)
                step(2, True, True, True)
                with act.Fori(3, STEPS - 1) as i:
                    step(i, True, True, True)
                step(STEPS - 1, False, True, True)
                turned_h(TILES - 2)
                stage(TILES - 1, GROUPS)
                turned_h(TILES - 1)
            with act.Else():
                with act.Fori(0, GROUPS) as g:
                    act.wait_ge(all_summed, g * TILES + 1)
                    nc.scalar.copy(idx[:, 0:GC], srci[:, bass.ds(g * GC, GC)]).then_inc(idx_ready, 1)
                stage(0, GROUPS * TILES + 1, all_added)
                turned_h(0)
                with act.Fori(1, TILES - 1) as t:
                    stage(t, GROUPS * TILES + 1, all_added)
                    turned_h(t)
                stage(TILES - 1, GROUPS * TILES + 1, all_added)
                turned_h(TILES - 1)

        @block.vector
        def _(dve):
            count = {"common": 0, "quick": 0, "general": 0}
            own = {"common": dve_step, "quick": dve_step_quick, "general": dve_step_general}

            def link(ins, path="common"):
                count[path] += 1
                ins.then_inc(own[path], 1)
                dve.wait_ge(own[path], count[path])

            V = nc.vector
            dve.wait_ge(dst_in, LIST_LOADS)
            V.tensor_copy(dst_f, dst_raw).then_inc(dst_float, 1)
            dve.wait_ge(consts, 7)
            link(V.tensor_copy(nodes[:, :], nodes_i[:, :]))
            V.tensor_single_scalar(lane_b[:, 0:CB], mask_i[:, 0:CB], CB - 1, ALU.bitwise_and)
            link(V.tensor_single_scalar(lane_i[:, 0:1], mask_i[:, 0:1], 2, ALU.logical_shift_right))
            V.tensor_tensor(diag[:, :], lane_b[:, 0:CB], nodes_i[0:64, 0:CB], ALU.is_equal)
            V.tensor_tensor(pick[:, :], lane_i[:, 0:1].broadcast_to([64, DB]), nodes_i[0:64, 0:DB], ALU.is_equal)
            link(V.memset(cnt[:, :], 0.0))

            rel_v = rel[:, :].rearrange("p (s j) -> p j s", j=SPC)
            first_v = first[:, :].rearrange("p (s j) -> p j s", j=SPC)
            for k in range(4):
                dve.wait_ge(dst_turned, k + 1)
                last = V.tensor_tensor(rel_v[:, 4 * k:4 * k + 4, :],
                                       banks[k][:, 0:4 * STEPS].rearrange("p (j s) -> p j s", j=4),
                                       first_v[:, 4 * k:4 * k + 4, :], ALU.subtract)
            link(last)
            V.tensor_reduce(hi_lo[:, 0:1], rel[:, :], AX.X, ALU.max)
            link(V.tensor_reduce(hi_lo[:, 1:2], rel[:, :], AX.X, ALU.min))
            link(V.tensor_single_scalar(hi_lo[:, 1:2], hi_lo[:, 1:2], -1.0, ALU.mult))
            V.scalar_tensor_tensor(out=worst[:, :], in0=hi_lo[:, 0:1], scalar=-(WIN - 1.0), in1=hi_lo[:, 1:2],
                                   op0=ALU.add, op1=ALU.max).then_inc(worst_ready, 1)
            V.memset(rel[P // 2:P, REAL_CH - 1:REAL_CH], FAR)
            link(V.memset(rel[:, REAL_CH:CH], FAR))
            dve.wait_ge(worst_turned, 1)
            link(V.tensor_reduce(flag[0:1, 0:1], banks[1][0:1, 0:P], AX.X, ALU.max))
            V.tensor_single_scalar(flag_i[0:1, 0:1], flag[0:1, 0:1], 0.5, ALU.is_lt).then_inc(flag_ready, 1)

            def layernorm(i, path):
                s = slice(i * BT, (i + 1) * BT)
                dve.wait_ge(x_in[i], 16 if i < BATCHES - 1 else 32)
                for t in range(i * BT, (i + 1) * BT):
                    last = V.bn_stats(stats[:, t, :], xall[:, t, :])
                link(last, path)
                V.tensor_tensor(mean2[:, s], stats[:, s, 1], stats[:, s, 4], ALU.add)
                V.tensor_tensor(dif[:, s], stats[:, s, 1], stats[:, s, 4], ALU.subtract)
                link(V.tensor_tensor(var[:, s], stats[:, s, 2], stats[:, s, 5], ALU.add), path)
                V.tensor_scalar(var[:, s], var[:, s], 1.0 / D, EPS, ALU.mult, ALU.add)
                link(V.scalar_tensor_tensor(out=dif[:, s], in0=dif[:, s], scalar=0.25, in1=dif[:, s],
                                            op0=ALU.mult, op1=ALU.mult), path)
                V.tensor_tensor(var[:, s], var[:, s], dif[:, s], ALU.add).then_inc(var_ready, 1)

            def layernorm_end(i, path):
                s = slice(i * BT, (i + 1) * BT)
                dve.wait_ge(std_ready, i + 1)
                link(V.reciprocal(rstd[:, s], std[:, s]), path)
                V.scalar_tensor_tensor(out=nmr[:, s], in0=mean2[:, s], scalar=-0.5, in1=rstd[:, s],
                                       op0=ALU.mult, op1=ALU.mult).then_inc(ln_ready, 1)

            quick = flag_value(dve)
            with dve.If(quick == 1):
                link(V.tensor_tensor(n_i.rearrange("p (g j) -> p g j", j=GC),
                                     rel[:, :].rearrange("p (g j) -> p g j", j=GC),
                                     j8[:, :].unsqueeze(1).broadcast_to([P, GROUPS, GC]), ALU.add), "quick")
                V.tensor_single_scalar(lo_i, n_i, DB - 1, ALU.bitwise_and)
                link(V.tensor_single_scalar(hi_i, n_i, 4, ALU.arith_shift_right), "quick")
                V.tensor_copy(digit_b, lo_i)
                link(V.tensor_copy(digit_a, hi_i), "quick")

                def cut_pass(i):
                    bank = banks[2 + i % 2]
                    dve.wait_ge(counted, i + 1)
                    link(V.tensor_tensor(cut[:, :].rearrange("p (q c) -> p q c", c=CB),
                                         bank[0:64, 0:PW * CB].rearrange("p (q c) -> p q c", c=CB),
                                         diag[:, :].unsqueeze(1).broadcast_to([64, PW, CB]), ALU.mult), "quick")
                    link(V.tensor_reduce(part[:, :], cut[:, :].rearrange("p (q c) -> p q c", c=CB), AX.X, ALU.add), "quick")
                    q0 = i * (PC // GC) * 4
                    V.tensor_tensor(cnt[:, q0:q0 + PW], cnt[:, q0:q0 + PW], part[:, :], ALU.add).then_inc(cnt_added, 1)
                    dve.wait_ge(cnt_added, i + 1)

                for i in range(PASSES):
                    if i:
                        dve.wait_ge(counted, i)
                    cs = slice(i * PC, (i + 1) * PC)
                    for v in range(DB):
                        V.tensor_single_scalar(hot_b[:, :, v, :], digit_b[:, cs].rearrange("p (m c) -> p m c", c=CB), float(v), ALU.is_equal)
                    for v in range(DA):
                        last = V.tensor_single_scalar(hot_a[:, :, v, :], digit_a[:, cs].rearrange("p (m c) -> p m c", c=CB), float(v), ALU.is_equal)
                    last.then_inc(hot_ready, 1)
                    if i:
                        cut_pass(i - 1)
                        layernorm_end(i - 1, "quick")
                    layernorm(i, "quick")
                cut_pass(PASSES - 1)
                layernorm_end(BATCHES - 1, "quick")
                dve.wait_ge(cnt_turned, 1)
                V.tensor_copy(deg_sb[0:QB, 0:PASSES * DB], banks[6][0:QB, 0:PASSES * DB]).then_inc(deg_ready, 1)
            with dve.Else():
                link(V.tensor_tensor(n_i, rel[:, :], first[:, :], ALU.add), "general")
                V.tensor_single_scalar(lo_i, n_i, P - 1, ALU.bitwise_and)
                link(V.tensor_single_scalar(hi_i, n_i, 7, ALU.arith_shift_right), "general")
                V.tensor_copy(lo_f, lo_i)
                link(V.tensor_copy(hi_f, hi_i), "general")
                for i in range(BATCHES):
                    layernorm(i, "general")
                    layernorm_end(i, "general")
                with dve.Fori(0, GROUPS) as g:
                    dve.wait_ge(all_counted, g + 1)
                    for j in range(GC):
                        V.tensor_scalar(hot_lo[:, j, :], nodes[:, :], lo_f[:, bass.ds(g * GC + j, 1)], None, ALU.is_equal)
                        last = V.tensor_scalar(hot_hi[:, j, :], nodes[:, :], hi_f[:, bass.ds(g * GC + j, 1)], None, ALU.is_equal)
                    last.then_inc(all_hot_ready, 1)
                dve.wait_ge(all_counted, GROUPS + 1)
                V.tensor_copy(deg_sb[0:TILES, :], banks[2][0:TILES, 0:P]).then_inc(deg_ready, 1)

            dve.wait_ge(deg_back, 16)
            V.tensor_single_scalar(deg_t[:, :], deg_t[:, :], 1.0, ALU.max).then_inc(deg_clamped, 1)
            dve.wait_ge(root_ready, 1)
            V.reciprocal(norm_t[:, :], root_t[:, :]).then_inc(norm_rows, 1)
            dve.wait_ge(norm_turned, 1)
            V.tensor_copy(norm[:, :], banks[7][:, 0:TILES]).then_inc(norm_ready, 1)
            dve.wait_ge(norm_ready, 1)
            for i in range(BATCHES):
                dve.wait_ge(h_ready, i + 1)
                for t in range(i * BT, (i + 1) * BT):
                    V.tensor_scalar(H[:, t, 0:D], H[:, t, 0:D], norm[:, t:t + 1], None, ALU.mult)
                V.tensor_copy(H[:, i * BT:(i + 1) * BT, D:ROW],
                              norm[:, i * BT:(i + 1) * BT].unsqueeze(2).broadcast_to([P, BT, ROW - D])).then_inc(rows_ready, 1)

            def finish(t):
                r = rows_of(t)
                dve.wait_ge(fin_mm, t + 1)
                dve.wait_ge(x_loaded, 16 * (t + 1))
                V.scalar_tensor_tensor(out=t1[0:r, :], in0=SELF[0:r, 0:D], scalar=FIN[0:r, D:D + 1], in1=x_st[0:r, :],
                                       op0=ALU.mult, op1=ALU.add).then_inc(t1_done, 1)
                dve.wait_ge(t1_done, t + 1)
                wait_prior(dve, stored, 16 * t)
                V.scalar_tensor_tensor(out=o_st[0:r, :], in0=FIN[0:r, 0:D], scalar=norm[0:r, bass.ds(t, 1)],
                                       in1=t1[0:r, :], op0=ALU.mult, op1=ALU.add).then_inc(out_ready, 1)

            dve.wait_ge(sums_clear, 2)
            with dve.If(quick == 1):
                def hots(i, half, k, prior):
                    for j in range(half * GC, half * GC + k):
                        if prior and j % 4 == 0:
                            dve.wait_ge(chunk_used, (i - 1) * SPC + j + 4)
                        V.tensor_scalar(OH[:, j, :], nodes[:, :], rel[:, bass.ds(i * SPC + j, 1)], None,
                                        ALU.is_equal).then_inc(hot, 1)

                def add(g, half, k=GC, prior=True):
                    w = WIN + NPC * (k - 1)
                    at = g * (NPC * GC) + PAD - BACK
                    dve.wait_ge(chunk_used, g * GC + k)
                    if prior:
                        dve.wait_ge(group_added, g)
                    V.tensor_tensor(AG[:, bass.ds(at, w)], AG[:, bass.ds(at, w)], agg_ps[half][:, 0:w], ALU.add)
                    V.tensor_tensor(SR[SP_ROW:SP_ROW + 1, bass.ds(at, w)], SR[SP_ROW:SP_ROW + 1, bass.ds(at, w)],
                                    s_ps[half][SP_ROW:SP_ROW + 1, 0:w], ALU.add).then_inc(group_added, 1)

                def step(i, k, prior, last_add, fin):
                    hots(i, 0, min(k, GC), prior)
                    if last_add:
                        add(2 * i - 1, 1)
                    hots(i, 1, k - GC, prior)
                    if fin:
                        finish(i - 2)
                    add(2 * i, 0, GC, last_add)

                step(0, SPC, False, False, False)
                step(1, SPC, True, True, False)
                step(2, SPC, True, True, True)
                with dve.Fori(3, STEPS - 1) as i:
                    step(i, SPC, True, True, True)
                step(STEPS - 1, LAST_CH, True, True, True)
                add(GROUPS - 1, 1, LAST_CH - GC)
                finish(TILES - 2)
                finish(TILES - 1)
            with dve.Else():
                for primed in (all_hot, all_added, grel_ready):
                    dve.sem_inc(primed)
                with dve.Fori(0, GROUPS) as g:
                    dve.wait_ge(all_hot, g * TILES + 1)
                    dve.wait_ge(grel_ready, g * (TILES + 1) + 1)
                    V.tensor_tensor(grel[:, :], rel[:, bass.ds(g * GC, GC)], first[:, bass.ds(g * GC, GC)],
                                    ALU.add).then_inc(grel_ready, 1)
                    with dve.Fori(0, TILES) as w:
                        visit = g * TILES + w
                        dve.wait_ge(grel_ready, visit + g + 2)
                        dve.wait_ge(all_summed, visit + 1)
                        for j in range(GC):
                            last = V.tensor_scalar(OH[:, j, :], nodes[:, :], grel[:, j:j + 1], None, ALU.is_equal)
                        last.then_inc(all_hot, 1)
                        dve.wait_ge(all_hot, visit + 2)
                        V.tensor_single_scalar(grel[:, :], grel[:, :], -float(P), ALU.add).then_inc(grel_ready, 1)
                        dve.wait_ge(all_summed, visit + 2)
                        dve.wait_ge(all_added, visit + 1)
                        at = w * P + PAD
                        V.tensor_tensor(AG[:, bass.ds(at, P)], AG[:, bass.ds(at, P)], AGG_A[:, 0:P], ALU.add)
                        V.tensor_tensor(SR[SP_ROW:SP_ROW + 1, bass.ds(at, P)], SR[SP_ROW:SP_ROW + 1, bass.ds(at, P)],
                                        S_A[SP_ROW:SP_ROW + 1, 0:P], ALU.add).then_inc(all_added, 1)
                finish(0)
                with dve.Fori(1, TILES - 1) as t:
                    finish(t)
                finish(TILES - 1)

        @block.tensor
        def _(pe):
            T = nc.tensor
            pe.wait_ge(consts, 7)
            pe.wait_ge(dst_float, 1)
            for k in range(SPC):
                last = T.transpose(banks[k // 4][:, (k % 4) * STEPS:(k % 4 + 1) * STEPS], dst_f[:, k * P:(k + 1) * P],
                                   ident[0:STEPS, 0:STEPS])
                if k % 4 == 3:
                    last.then_inc(dst_turned, 1)
            pe.wait_ge(w_loaded, 32)
            for k in range(2):
                last = T.transpose(banks[4][:, k * D:(k + 1) * D], w_in[:, k * D:(k + 1) * D], ident[:, :])
            last.then_inc(w_turned, 1)
            pe.wait_ge(worst_ready, 1)
            T.transpose(banks[1][0:1, 0:P], worst[:, :], ident[:, :]).then_inc(worst_turned, 1)
            pe.wait_ge(w_ready, 1)
            pe.wait_ge(src_float, 1)
            for k in range(SPC):
                last = T.transpose(banks[4 + k // 4][:, (k % 4) * STEPS:(k % 4 + 1) * STEPS],
                                   src_f[:, k * P:(k + 1) * P], ident[0:STEPS, 0:STEPS])
                if k % 4 == 3:
                    last.then_inc(src_turned, 1)

            quick = flag_value(pe)
            with pe.If(quick == 1):
                for i in range(PASSES):
                    pe.wait_ge(hot_ready, i + 1)
                    for m in range(PC // CB):
                        q0 = (m * CB // GC) * 4
                        last = T.matmul(banks[2 + i % 2][0:64, q0 * CB:(q0 + DA) * CB], hot_b[:, m].rearrange("p v c -> p (v c)"),
                                        hot_a[:, m].rearrange("p v c -> p (v c)"), start=(m == 0), stop=(m == PC // CB - 1),
                                        skip_group_check=True)
                    last.then_inc(counted, 1)
                pe.wait_ge(cnt_added, PASSES)
                pe.wait_ge(src_ready, 1)
                for k in range(PASSES):
                    q0 = PAD // DB + k * QB
                    last = T.matmul(banks[6][0:QB, k * DB:(k + 1) * DB], cnt[:, q0:q0 + QB], pick[:, :],
                                    start=True, stop=True)
                last.then_inc(cnt_turned, 1)
            with pe.Else():
                pe.sem_inc(all_counted)
                def count_group(g, start):
                    pe.wait_ge(all_hot_ready, g + 1)
                    for j in range(GC):
                        last = T.matmul(banks[2][:, 0:P], hot_hi[:, j, :], hot_lo[:, j, :],
                                        start=start and j == 0, stop=False, skip_group_check=True)
                    last.then_inc(all_counted, 1)

                count_group(0, True)
                with pe.Fori(1, GROUPS) as g:
                    count_group(g, False)

            pe.wait_ge(norm_rows, 1)
            pe.wait_ge(src_ready, 1)
            T.transpose(banks[7][:, 0:TILES], norm_t[:, :], ident[0:TILES, 0:TILES]).then_inc(norm_turned, 1)

            def turn_tile(t):
                r = rows_of(t)
                pe.wait_ge(h_loaded, 16 * (t + 1))
                T.transpose(TURN[:, 0:r], h_st[0:r, 0:D], ident[0:r, 0:r]).then_inc(h_turned, 1)

            def finish_tile(t):
                r = rows_of(t)
                pe.wait_ge(hT_ready, t + 1)
                pe.wait_ge(staged, t + 1)
                wait_prior(pe, out_ready, t)
                T.matmul(SELF[0:r, 0:D], hT[:, 0:r], wT[:, 0:D], start=True, stop=True)
                T.matmul(FIN[0:r, 0:D + 1], s_st[0:1, 0:r], brow[0:1, :], start=True, stop=False, skip_group_check=True)
                T.matmul(FIN[0:r, 0:D], a_st[:, 0:r], wT[:, D:2 * D], start=False, stop=True,
                         skip_group_check=True).then_inc(fin_mm, 1)

            def sum_chunk(agg, s_out, j, start, stop):
                T.matmul(agg, G[:, j, 0:D], OH[:, j, :], start=start, stop=stop, skip_group_check=True)
                return T.matmul(s_out, G[:, j, D - SP_ROW:D + 1], OH[:, j, :], start=start, stop=stop, skip_group_check=True)

            pe.wait_ge(w_ready, 1)
            with pe.If(quick == 1):
                def step(i, k, turn, adds):
                    for j in range(k):
                        half, jj = j // GC, j % GC
                        if jj == 0 and adds:
                            pe.wait_ge(group_added, 2 * i - 1 + half)
                        pe.wait_ge(landed[j], 16 * (i + 1))
                        pe.wait_ge(hot, i * SPC + j + 1)
                        c0 = NPC * jj
                        stop = jj == GC - 1 or j == k - 1
                        last = sum_chunk(agg_ps[half][:, c0:c0 + WIN],
                                         s_ps[half][0:SP_ROW + 1, c0:c0 + WIN], j, jj == 0, stop)
                        last.then_inc(chunk_used, 1)
                        if turn and j == 0:
                            turn_tile(i - 2)
                        if turn and j == 3:
                            finish_tile(i - 2)

                step(0, SPC, False, False)
                step(1, SPC, False, True)
                step(2, SPC, True, True)
                with pe.Fori(3, STEPS - 1) as i:
                    step(i, SPC, True, True)
                step(STEPS - 1, LAST_CH, True, True)
                for t in (TILES - 2, TILES - 1):
                    turn_tile(t)
                    finish_tile(t)
            with pe.Else():
                pe.sem_inc(all_summed)
                with pe.Fori(0, GROUPS) as g:
                    for j in range(GC):
                        pe.wait_ge(landed[j], 16 * (g + 1))
                    pe.sem_inc(waited)
                    with pe.Fori(0, TILES) as w:
                        visit = g * TILES + w
                        pe.wait_ge(all_added, visit + 1)
                        pe.wait_ge(all_hot, visit + 2)
                        for j in range(GC):
                            last = sum_chunk(AGG_A[:, 0:P], S_A[0:SP_ROW + 1, 0:P], j, j == 0, j == GC - 1)
                        last.then_inc(all_summed, 1)
                turn_tile(0)
                finish_tile(0)
                with pe.Fori(1, TILES - 1) as t:
                    turn_tile(t)
                    finish_tile(t)
                turn_tile(TILES - 1)
                finish_tile(TILES - 1)


def kernel(x, src, dst, L0_gnn_W, L0_gnn_b):
    import numpy as np
    import concourse.bacc as bacc
    from concourse.bass_utils import run_bass_kernel_spmd

    nc = bacc.Bacc("TRN2", target_bir_lowering=False, num_devices=1)
    arrays, args = {}, []
    for name, a in (("x", x), ("src", src), ("dst", dst), ("W", L0_gnn_W), ("b", L0_gnn_b)):
        a = np.ascontiguousarray(a)
        arrays[f"in_{name}"] = a
        args.append(nc.dram_tensor(f"in_{name}", a.shape, mybir.dt.from_np(a.dtype), kind="ExternalInput").ap())
    out = nc.dram_tensor("out_nodes", args[0].shape, mybir.dt.float32, kind="ExternalOutput").ap()
    gnn_layer(nc, *args, out)
    r = run_bass_kernel_spmd(nc, [arrays], core_ids=[0])
    return r.results[0]["out_nodes"]
```

```python
import concourse.bass as bass
from concourse import mybir
from contextlib import ExitStack


def gnn_layer(nc, x, src, dst, W, b, out):
    f32, bf16, i32 = mybir.dt.float32, mybir.dt.bfloat16, mybir.dt.int32
    ALU = mybir.AluOpType
    ACT = mybir.ActivationFunctionType
    AX = mybir.AxisListType

    N, D = x.shape
    E = src.shape[0]
    P = 128
    TILES = -(-N // P)
    LAST_ROWS = N - (TILES - 1) * P
    SPC = 16
    STEP_E = SPC * P
    STEPS = -(-E // STEP_E)
    CH = STEPS * SPC
    REAL_CH = -(-E // P)
    LAST_CH = REAL_CH - (STEPS - 1) * SPC
    FULL_ROWS = E // STEP_E
    LIST_LOADS = 48 if FULL_ROWS >= 16 else 32
    TAIL_E = E - FULL_ROWS * STEP_E
    NPC = N * P // E
    GC = 8
    GROUPS = CH // GC
    WIN = P
    BACK = (WIN - NPC) // 2
    GW = WIN + NPC * (GC - 1)
    PAD = P // 2
    COLS = TILES * P + 2 * PAD
    ROW = D + 4
    EPS = 1e-5
    FAR = -32768.0
    BATCHES = 7
    PASSES = 7
    CUTS = [0] + [TILES // PASSES * (i + 1) - 1 for i in range(PASSES - 1)] + [TILES]
    ORDER = [6, 5, 0, 1, 2, 3, 4]
    EARLY = [6, 5]
    STAT_GROUPS = [(CUTS[5], CUTS[7]), (CUTS[0], CUTS[2]), (CUTS[2], CUTS[4]), (CUTS[4], CUTS[5])]
    DB, DA = 16, 12
    CB = 4
    PC = CH // PASSES
    PW = (PC // GC - 1) * 4 + DA
    HOT_PASSES = [(0, 2), (2, 4), (4, 6), (6, 7)]
    HPC = 2 * PC
    Q = COLS // DB
    TQ = P // DB
    assert D == P and NPC == 8 and STEPS == TILES and TILES % PASSES == 0 and CH == PASSES * PC
    assert E % P == P // 2 and PAD % DB == 0
    assert PAD + TILES * P <= COLS and (GROUPS - 1) * NPC * GC + PAD - BACK + GW <= COLS

    row_of = lambda a, t, k: a[t * P:(t + k) * P, :].rearrange("(t p) d -> p t d", p=P)

    table = nc.dram_tensor("table", (TILES * P, ROW), f32, kind="Internal").ap()

    ctx = ExitStack()
    with ctx:
        sb = lambda name, shape, dt: ctx.enter_context(nc.sbuf_tensor(name, shape, dt))
        sem = lambda name: ctx.enter_context(nc.semaphore(name))
        banks = [ctx.enter_context(nc.psum_tensor(f"bank{i}", [P, 512], f32)) for i in range(8)]

        AG = sb("AG", [P, COLS], f32)
        SR = sb("SR", [P, COLS], f32)
        HT = sb("HT", [P, TILES * ROW], f32)
        xall = AG[:, 0:TILES * P].rearrange("p (t d) -> p t d", d=D)
        H = HT[:, :].rearrange("p (t r) -> p t r", r=ROW)
        SP_ROW = 96
        raw0 = TILES * ROW - 5 * STEP_E
        dst_raw, dst_f, src_raw, src_f, digits_raw = (
            HT[0:STEPS, raw0 + i * STEP_E:raw0 + (i + 1) * STEP_E] for i in range(5))
        dst_raw, src_raw = dst_raw.bitcast(i32), src_raw.bitcast(i32)
        b_raw = digits_raw[:, 0:STEP_E // 2].bitcast(bf16)
        a_raw = digits_raw[:, STEP_E // 2:STEP_E].bitcast(bf16)
        rel = sb("rel", [P, CH], f32)
        srci = sb("srci", [P, CH], i32)
        first = sb("first", [P, CH], i32)
        a_first = sb("a_first", [P, 2], f32)
        a_first_i = sb("a_first_i", [P, 2], i32)
        ident_b = sb("ident_b", [P, P], bf16)
        nodes = sb("nodes", [P, WIN], f32)
        nodes_i = sb("nodes_i", [P, WIN], i32)
        ident = sb("ident", [P, P], f32)
        w_in = sb("w_in", [P, 2 * D], f32)
        wT = sb("wT", [P, 2 * D], f32)
        brow = sb("brow", [1, D + 1], f32)
        stats = sb("stats", [P, TILES, 6], f32)
        mean2 = sb("mean2", [P, TILES], f32)
        dif = sb("dif", [P, TILES], f32)
        var = sb("var", [P, TILES], f32)
        std = sb("std", [P, TILES], f32)
        rstd = sb("rstd", [P, TILES], f32)
        nmr = sb("nmr", [P, TILES], f32)
        scl = sb("scl", [P, TILES], f32)
        off = sb("off", [P, TILES], f32)
        edge_of_window = sb("edge_of_window", [P, 1], f32)
        outside = sb("outside", [P, 3], f32)
        flag = sb("flag", [1, 2], f32)
        flag_i = sb("flag_i", [1, 1], i32)
        mask_i = sb("mask_i", [64, 1], i32)
        lane_b = sb("lane_b", [64, 1], i32)
        diag = sb("diag", [64, CB], f32)
        pick = sb("pick", [64, 2 * P - DB], f32)
        pick_i = sb("pick_i", [64, 2 * P - DB], i32)
        row_i = sb("row_i", [64, 1], i32)
        own = sb("own", [64, PW, CB], f32)
        part = sb("part", [64, PW], f32)
        cnt = sb("cnt", [64, Q], f32)
        deg_sb = sb("deg_sb", [P, P], f32)
        deg = sb("deg", [P, TILES], f32)
        root = sb("root", [P, TILES], f32)
        norm = sb("norm", [P, TILES], f32)
        idx = sb("idx", [P, SPC], i32)
        GO = sb("GO", [P, SPC * (ROW + WIN)], f32)
        G = GO[:, 0:SPC * ROW].rearrange("p (j r) -> p j r", r=ROW)
        OH = GO[:, SPC * ROW:SPC * (ROW + WIN)].rearrange("p (j n) -> p j n", n=WIN)
        waste = GO[:, 0:CH // 2].bitcast(bf16)
        h_st = sb("h_st", [P, ROW], f32)
        x_st = sb("x_st", [P, D], f32)
        a_st = sb("a_st", [P, P], f32)
        s_st = sb("s_st", [1, P], f32)
        hT = sb("hT", [P, P], f32)
        t1 = sb("t1", [P, D], f32)
        o_st = sb("o_st", [P, D], f32)
        grel = sb("grel", [P, GC], f32)

        scr = SR[:, :]
        digit_b = scr[:, 0:CH // 2].bitcast(bf16)
        digit_a = scr[:, CH // 2:CH].bitcast(bf16)
        hot_b = scr[:, CH:CH + DB * HPC // 2].bitcast(bf16).rearrange("p (m v c) -> p m v c", m=HPC // CB, c=CB)
        o0 = CH + DB * HPC // 2
        hot_a = scr[:, o0:o0 + DA * HPC // 2].bitcast(bf16).rearrange("p (m v c) -> p m v c", m=HPC // CB, c=CB)
        o0 += DA * HPC // 2
        b_i, a_i = (scr[0:STEPS, o0 + i * STEP_E:o0 + (i + 1) * STEP_E].bitcast(i32) for i in range(2))
        n_i, lo_i, hi_i = (scr[:, i * CH:(i + 1) * CH].bitcast(i32) for i in range(3))
        lo_f, hi_f = (scr[:, i * CH:(i + 1) * CH] for i in range(3, 5))
        o1 = 5 * CH
        hot_lo = scr[:, o1:o1 + GC * P // 2].bitcast(bf16).rearrange("p (j n) -> p j n", j=GC)
        hot_hi = scr[:, o1 + GC * P // 2:o1 + GC * P].bitcast(bf16).rearrange("p (j n) -> p j n", j=GC)

        dst_in = sem("dst_in")
        src_in = sem("src_in")
        x_in = [sem(f"x_in{i}") for i in range(BATCHES)]
        w_loaded = sem("w_loaded")
        edge_pads = sem("edge_pads")
        consts = sem("consts")
        pool_step = sem("pool_step")
        outside_summed = sem("outside_summed")
        own_general = sem("own_general")
        dve_step = sem("dve_step")
        act_step = sem("act_step")
        dst_float = sem("dst_float")
        src_float = sem("src_float")
        w_turned = sem("w_turned")
        w_ready = sem("w_ready")
        dst_turned = sem("dst_turned")
        src_turned = sem("src_turned")
        src_ready = sem("src_ready")
        flag_ready = sem("flag_ready")
        b_split = sem("b_split")
        a_split = sem("a_split")
        digits_float = sem("digits_float")
        digits_turned = sem("digits_turned")
        digits_ready = sem("digits_ready")
        rel_ready = sem("rel_ready")
        outside_ready = sem("outside_ready")
        outside_turned = sem("outside_turned")
        deg_turned = sem("deg_turned")
        rows_counted = sem("rows_counted")
        bank_nodes = sem("bank_nodes")
        hot_ready = sem("hot_ready")
        counted = sem("counted")
        cnt_added = sem("cnt_added")
        grel_ready = sem("grel_ready")
        all_hot = sem("all_hot")
        all_summed = sem("all_summed")
        all_added = sem("all_added")
        all_counted = sem("all_counted")
        all_hot_ready = sem("all_hot_ready")
        dve_step_quick = sem("dve_step_quick")
        dve_step_general = sem("dve_step_general")
        deg_ready = sem("deg_ready")
        pre_ready = sem("pre_ready")
        scale_ready = sem("scale_ready")
        act_rows = sem("act_rows")
        dve_rows = sem("dve_rows")
        cnt_clear = sem("cnt_clear")
        all_norm = sem("all_norm")
        all_scaled = sem("all_scaled")
        all_rows = sem("all_rows")
        table_again = sem("table_again")
        tile_again = sem("tile_again")
        consts_float = sem("consts_float")
        root_ready = sem("root_ready")
        var_ready = sem("var_ready")
        std_ready = sem("std_ready")
        ln_ready = sem("ln_ready")
        table_done = sem("table_done")
        sums_clear = sem("sums_clear")
        idx_ready = sem("idx_ready")
        waited = sem("waited")
        landed = [sem(f"landed{i}") for i in range(SPC)]
        hot = sem("hot")
        chunk_used = sem("chunk_used")
        group_added = sem("group_added")
        h_loaded = sem("h_loaded")
        x_loaded = sem("x_loaded")
        h_turned = sem("h_turned")
        hT_ready = sem("hT_ready")
        staged = sem("staged")
        fin_mm = sem("fin_mm")
        t1_done = sem("t1_done")
        out_ready = sem("out_ready")
        stored = sem("stored")

        AGG_A, AGG_B, S_A, S_B, TURN, SELF, FIN, NODES = banks
        agg_ps, s_ps = [AGG_A, AGG_B], [S_A, S_B]

        def wait_prior(eng, what, value):
            if not (isinstance(value, int) and value == 0):
                eng.wait_ge(what, value)

        def rows_of(t):
            return LAST_ROWS if isinstance(t, int) and t == TILES - 1 else P

        def flag_value(eng):
            eng.wait_ge(flag_ready, 1)
            return eng.value_load(flag_i[0:1, 0:1], min_val=0, max_val=1)

        block = ctx.enter_context(nc.Block())

        @block.sync
        def _(sp):
            def load_list(raw, lst, list_in, pads):
                k = FULL_ROWS // 16 * 16
                if k:
                    sp.dma_start(raw[0:k, :], lst[0:k * STEP_E].rearrange("(s e) -> s e", e=STEP_E)).then_inc(list_in, 16)
                sp.wait_ge(edge_pads, pads)
                sp.dma_start(raw[k:FULL_ROWS, :], lst[k * STEP_E:FULL_ROWS * STEP_E].rearrange("(s e) -> s e", e=STEP_E)).then_inc(list_in, 16)
                sp.dma_start(raw[FULL_ROWS:STEPS, 0:TAIL_E], lst[FULL_ROWS * STEP_E:E].rearrange("(s e) -> s e", s=1)).then_inc(list_in, 16)

            load_list(dst_raw, dst, dst_in, 1)
            for i in ORDER:
                t0, t1 = CUTS[i], min(CUTS[i + 1], TILES - 1)
                sp.dma_start(xall[:, t0:t1, :], row_of(x, t0, t1 - t0)).then_inc(x_in[i], 16)
                if t1 == TILES - 1:
                    sp.wait_ge(consts, 1)
                    sp.dma_start(xall[0:LAST_ROWS, TILES - 1, :], x[(TILES - 1) * P:N, :]).then_inc(x_in[i], 16)
                if i == 6:
                    load_list(src_raw, src, src_in, 2)
            sp.dma_start(w_in[:, :], W).then_inc(w_loaded, 16)
            sp.dma_start(brow[0:1, 0:D], b.rearrange("(a d) -> a d", a=1)).then_inc(w_loaded, 16)

            for i, rows, n in ((0, act_rows, 1), (1, act_rows, 2), (2, act_rows, 3), (3, act_rows, 4),
                               (5, dve_rows, 1), (4, act_rows, 5), (6, dve_rows, 2)):
                sp.wait_ge(rows, n)
                sp.dma_start(row_of(table, CUTS[i], CUTS[i + 1] - CUTS[i]), H[:, CUTS[i]:CUTS[i + 1], :]).then_inc(table_done, 16)
            sp.wait_ge(table_done, 16 * BATCHES)
            quick = flag_value(sp)
            with sp.If(quick == 0):
                sp.wait_ge(all_rows, 1)
                sp.dma_start(row_of(table, 0, TILES), H).then_inc(table_again, 16)
                sp.wait_ge(table_again, 16)

            def load_rows(t):
                r = rows_of(t)
                wait_prior(sp, h_turned, t)
                sp.dma_start(h_st[0:r, :], table[bass.ds(t * P, r), :]).then_inc(h_loaded, 16)
                wait_prior(sp, t1_done, t)
                sp.dma_start(x_st[0:r, :], x[bass.ds(t * P, r), :]).then_inc(x_loaded, 16)

            def store_rows(t):
                r = rows_of(t)
                sp.wait_ge(out_ready, t + 1)
                sp.dma_start(out[bass.ds(t * P, r), :], o_st[0:r, :]).then_inc(stored, 16)

            load_rows(0)
            with sp.Fori(0, TILES - 2) as t:
                load_rows(t + 1)
                store_rows(t)
            load_rows(TILES - 1)
            store_rows(TILES - 2)
            store_rows(TILES - 1)
            sp.wait_ge(stored, 16 * TILES)

        @block.gpsimd
        def _(pool):
            tail = slice(FULL_ROWS // 32 * 32, STEPS)
            pool.memset(dst_raw[tail, TAIL_E:STEP_E], N - 1).then_inc(edge_pads, 1)
            pool.wait_ge(edge_pads, 1)
            pool.memset(src_raw[tail, TAIL_E:STEP_E], 0).then_inc(edge_pads, 1)
            pool.wait_ge(edge_pads, 2)
            pool.memset(xall[:, TILES - 1, :], 0.0).then_inc(consts, 1)
            pool.memset(ident[:, :], 0.0).then_inc(pool_step, 1)
            pool.wait_ge(pool_step, 1)
            pool.affine_select(out=ident[:, :], in_=ident[:, :], compare_op=ALU.not_equal, fill=1.0, base=0,
                               pattern=[[-1, P]], channel_multiplier=1).then_inc(consts, 1)
            pool.iota(a_first_i[:, :], pattern=[[-NPC * GC // DB, 2]], base=PAD // DB,
                      channel_multiplier=-2 * NPC * GC // DB).then_inc(consts, 1)
            pool.iota(nodes_i[:, :], pattern=[[1, WIN]], base=0, channel_multiplier=0).then_inc(consts, 1)
            pool.iota(first[:, :], pattern=[[NPC, CH]], base=-BACK, channel_multiplier=0).then_inc(consts, 1)
            pool.wait_ge(consts, 5)
            pool.iota(mask_i[:, :], pattern=[[0, 1]], base=0, channel_multiplier=1).then_inc(consts, 1)
            pool.wait_ge(consts, 6)
            pool.iota(pick_i[:, :], pattern=[[1, 2 * P - DB]], base=-(P - DB), channel_multiplier=0).then_inc(consts, 1)
            pool.wait_ge(consts, 7)
            pool.memset(brow[0:1, D:D + 1], 1.0).then_inc(consts, 1)
            pool.wait_ge(consts, 8)
            pool.memset(cnt[:, :], 0.0).then_inc(cnt_clear, 1)
            pool.wait_ge(cnt_clear, 1)
            pool.wait_ge(dst_in, LIST_LOADS)
            pool.tensor_copy(dst_f, dst_raw).then_inc(dst_float, 1)
            pool.wait_ge(dst_float, 1)
            pool.wait_ge(src_in, LIST_LOADS)
            pool.tensor_copy(src_f, src_raw).then_inc(src_float, 1)

            quick = flag_value(pool)
            pool.wait_ge(table_done, 16 * BATCHES)

            def gather(j):
                pool.indirect_dma_start(G[:, j, :], None, table[:, :],
                                        bass.IndirectOffsetOnAxis(ap=idx[:, j:j + 1], axis=0)).then_inc(landed[j], 16)

            with pool.If(quick == 1):
                def step(i, k, prior):
                    for j in range(k):
                        if j % GC == 0:
                            pool.wait_ge(idx_ready, 2 * i + j // GC + 1)
                            pool.sem_inc(waited)
                        if prior and j % 4 == 0:
                            pool.wait_ge(chunk_used, (i - 1) * SPC + j + 4)
                            pool.sem_inc(waited)
                        gather(j)

                step(0, SPC, False)
                with pool.Fori(1, STEPS - 1) as i:
                    step(i, SPC, True)
                step(STEPS - 1, LAST_CH, True)
            with pool.Else():
                pool.wait_ge(table_again, 16)
                pool.wait_ge(all_rows, 1)
                pool.memset(AG[:, :], 0.0).then_inc(sums_clear, 1)
                pool.wait_ge(sums_clear, 1)
                pool.memset(SR[SP_ROW:SP_ROW + 1, :], 0.0).then_inc(sums_clear, 1)
                with pool.Fori(0, GROUPS) as g:
                    pool.wait_ge(idx_ready, g + 1)
                    pool.wait_ge(all_summed, g * TILES + 1)
                    pool.sem_inc(waited)
                    for j in range(GC):
                        gather(j)

        @block.scalar
        def _(act):
            act.wait_ge(b_split, 1)
            nc.scalar.copy(b_raw, b_i).then_inc(digits_float, 1)
            act.wait_ge(a_split, 1)
            act.wait_ge(consts_float, 1)
            for half in range(2):
                h = slice(half * STEP_E // 2, (half + 1) * STEP_E // 2)
                last = nc.scalar.activation(a_raw[:, h], a_i[:, h], ACT.Identity, bias=a_first[0:STEPS, half:half + 1])
            last.then_inc(digits_float, 1)
            for k in range(4):
                act.wait_ge(digits_turned, k + 1)
                digit = (digit_b, digit_a)[k // 2]
                last = nc.scalar.copy(digit.rearrange("p (s j) -> p j s", j=SPC)[:, 8 * (k % 2):8 * (k % 2) + 8, :],
                                      banks[k][:, :].bitcast(bf16)[:, 0:8 * STEPS].rearrange("p (j s) -> p j s", j=8))
            last.then_inc(digits_ready, 1)

            def deviations(g):
                s = slice(*STAT_GROUPS[g])
                act.wait_ge(var_ready, g + 1)
                nc.scalar.activation(std[:, s], var[:, s], ACT.Sqrt).then_inc(std_ready, 1)

            def roots(i, n):
                s = slice(CUTS[i], CUTS[i + n])
                act.wait_ge(deg_ready, i + n)
                nc.scalar.activation(root[:, s], deg[:, s], ACT.Sqrt).then_inc(root_ready, 1)

            def normalize(i, scale, offset, ready):
                for t in range(CUTS[i], CUTS[i + 1]):
                    last = nc.scalar.activation(H[:, t, 0:D], xall[:, t, :], ACT.Relu,
                                                scale=scale[:, t:t + 1], bias=offset[:, t:t + 1])
                last.then_inc(ready, 1)

            deviations(0)
            for k in range(4):
                act.wait_ge(src_turned, k + 1)
                last = nc.scalar.copy(
                    srci[:, :].rearrange("p (s j) -> p j s", j=SPC)[:, 4 * k:4 * k + 4, :],
                    banks[k][:, 0:4 * STEPS].rearrange("p (j s) -> p j s", j=4))
            last.then_inc(src_ready, 1)
            act.wait_ge(rel_ready, 1)
            nc.scalar.activation(waste, rel[:, :], ACT.Relu, bias=edge_of_window[:, :],
                                 accum_out=outside[:, 0:1]).then_inc(act_step, 1)
            act.wait_ge(act_step, 1)
            nc.scalar.activation(waste, rel[:, :], ACT.Relu, scale=-1.0,
                                 accum_out=outside[:, 1:2]).then_inc(outside_ready, 1)
            act.wait_ge(ln_ready, 1)
            act.wait_ge(dst_turned, 4)
            normalize(6, rstd, nmr, pre_ready)
            deviations(1)
            normalize(5, rstd, nmr, pre_ready)
            roots(0, 2)
            deviations(2)
            act.wait_ge(scale_ready, 1)
            normalize(0, scl, off, act_rows)
            normalize(1, scl, off, act_rows)
            roots(2, 2)
            deviations(3)
            act.wait_ge(scale_ready, 2)
            normalize(2, scl, off, act_rows)
            normalize(3, scl, off, act_rows)
            act.wait_ge(w_turned, 1)
            nc.scalar.copy(wT[:, :], banks[6][:, 0:2 * D]).then_inc(w_ready, 1)
            roots(4, 2)
            act.wait_ge(scale_ready, 3)
            normalize(4, scl, off, act_rows)
            roots(6, 1)

            quick = flag_value(act)
            act.wait_ge(src_ready, 1)

            def hand_idx(i, half):
                nc.scalar.copy(idx[:, half * GC:(half + 1) * GC],
                               srci[:, bass.ds(i * SPC + half * GC, GC)]).then_inc(idx_ready, 1)

            def turned_h(t):
                r = rows_of(t)
                act.wait_ge(h_turned, t + 1)
                nc.scalar.copy(hT[:, 0:r], TURN[:, 0:r]).then_inc(hT_ready, 1)

            def stage(t, adds, added=group_added):
                act.wait_ge(added, adds)
                wait_prior(act, fin_mm, t)
                nc.scalar.copy(a_st[:, :], AG[:, bass.ds(t * P + PAD, P)])
                nc.scalar.copy(s_st[:, :], SR[SP_ROW:SP_ROW + 1, bass.ds(t * P + PAD, P)]).then_inc(staged, 1)

            with act.If(quick == 1):
                def step(i, ahead, t_turn, t_stage, second_ahead=True):
                    if t_turn:
                        turned_h(i - 2)
                    if ahead:
                        act.wait_ge(chunk_used, i * SPC + GC)
                        hand_idx(i + 1, 0)
                    if t_stage:
                        stage(i - 1, 2 * i + 1)
                    if ahead:
                        act.wait_ge(chunk_used, (i + 1) * SPC)
                        hand_idx(i + 1, 1)

                hand_idx(0, 0)
                hand_idx(0, 1)
                step(0, True, False, False)
                step(1, True, False, True)
                step(2, True, True, True)
                with act.Fori(3, STEPS - 1) as i:
                    step(i, True, True, True)
                step(STEPS - 1, False, True, True)
                turned_h(TILES - 2)
                stage(TILES - 1, GROUPS)
                turned_h(TILES - 1)
            with act.Else():
                act.wait_ge(all_norm, 1)
                nc.scalar.activation(root[:, :], deg[:, :], ACT.Sqrt).then_inc(all_norm, 1)
                act.wait_ge(all_scaled, 1)
                act.wait_ge(table_done, 16 * BATCHES)
                with act.Fori(0, TILES) as t:
                    nc.scalar.activation(H[:, bass.ds(t, 1), 0:D].rearrange("p o d -> p (o d)"),
                                         xall[:, bass.ds(t, 1), :].rearrange("p o d -> p (o d)"), ACT.Relu,
                                         scale=scl[:, bass.ds(t, 1)], bias=off[:, bass.ds(t, 1)]).then_inc(tile_again, 1)
                act.wait_ge(tile_again, TILES)
                act.sem_inc(all_rows)
                with act.Fori(0, GROUPS) as g:
                    act.wait_ge(all_summed, g * TILES + 1)
                    nc.scalar.copy(idx[:, 0:GC], srci[:, bass.ds(g * GC, GC)]).then_inc(idx_ready, 1)
                stage(0, GROUPS * TILES + 1, all_added)
                turned_h(0)
                with act.Fori(1, TILES - 1) as t:
                    stage(t, GROUPS * TILES + 1, all_added)
                    turned_h(t)
                stage(TILES - 1, GROUPS * TILES + 1, all_added)
                turned_h(TILES - 1)

        @block.vector
        def _(dve):
            count = [0]

            def link(ins):
                count[0] += 1
                ins.then_inc(dve_step, 1)
                dve.wait_ge(dve_step, count[0])

            V = nc.vector
            dve.wait_ge(consts, 4)
            V.memset(edge_of_window[:, :], -(WIN - 1.0))
            V.tensor_copy(ident_b[:, :], ident[:, :])
            V.tensor_copy(nodes[:, :], nodes_i[:, :])
            V.tensor_copy(a_first[:, :], a_first_i[:, :]).then_inc(consts_float, 1)
            dve.wait_ge(dst_in, LIST_LOADS)
            V.tensor_single_scalar(b_i, dst_raw, DB - 1, ALU.bitwise_and).then_inc(b_split, 1)
            V.tensor_single_scalar(a_i, dst_raw, 4, ALU.logical_shift_right).then_inc(a_split, 1)

            def statistics(i):
                dve.wait_ge(x_in[i], 16 if i < BATCHES - 1 else 32)
                for t in range(CUTS[i], CUTS[i + 1]):
                    last = V.bn_stats(stats[:, t, :], xall[:, t, :])
                return last

            def variances(i):
                s = slice(*STAT_GROUPS[i])
                V.tensor_tensor(mean2[:, s], stats[:, s, 1], stats[:, s, 4], ALU.add)
                V.tensor_tensor(dif[:, s], stats[:, s, 1], stats[:, s, 4], ALU.subtract)
                link(V.tensor_tensor(var[:, s], stats[:, s, 2], stats[:, s, 5], ALU.add))
                V.tensor_scalar(var[:, s], var[:, s], 1.0 / D, EPS, ALU.mult, ALU.add)
                link(V.scalar_tensor_tensor(out=dif[:, s], in0=dif[:, s], scalar=0.25, in1=dif[:, s],
                                            op0=ALU.mult, op1=ALU.mult))
                V.tensor_tensor(var[:, s], var[:, s], dif[:, s], ALU.add).then_inc(var_ready, 1)

            def scales(i):
                s = slice(*STAT_GROUPS[i])
                dve.wait_ge(std_ready, i + 1)
                link(V.reciprocal(rstd[:, s], std[:, s]))
                V.scalar_tensor_tensor(out=nmr[:, s], in0=mean2[:, s], scalar=-0.5, in1=rstd[:, s],
                                       op0=ALU.mult, op1=ALU.mult).then_inc(ln_ready, 1)

            def hot_digits(n):
                p0, p1 = HOT_PASSES[n]
                if n:
                    dve.wait_ge(counted, p0)
                cs = slice(p0 * PC, p1 * PC)
                m = (p1 - p0) * PC // CB
                for v in range(DB):
                    V.tensor_single_scalar(hot_b[:, 0:m, v, :], digit_b[:, cs].rearrange("p (m c) -> p m c", c=CB), float(v), ALU.is_equal)
                for v in range(DA):
                    last = V.tensor_single_scalar(hot_a[:, 0:m, v, :], digit_a[:, cs].rearrange("p (m c) -> p m c", c=CB), float(v), ALU.is_equal)
                last.then_inc(hot_ready, 1)

            def cut_pass(i):
                q0 = i * (PC // GC) * 4
                dve.wait_ge(counted, i + 1)
                link(V.tensor_tensor(own[:, :, :], banks[4 + i % 2][0:64, 0:PW * CB].rearrange("p (q c) -> p q c", c=CB),
                                     diag[:, :].unsqueeze(1).broadcast_to([64, PW, CB]), ALU.mult))
                link(V.tensor_reduce(part[:, :], own[:, :, :], AX.X, ALU.add))
                if i:
                    dve.wait_ge(cnt_added, i)
                V.tensor_tensor(cnt[:, q0:q0 + PW], cnt[:, q0:q0 + PW], part[:, :], ALU.add).then_inc(cnt_added, 1)

            def degrees(i):
                dve.wait_ge(deg_turned, i + 1)
                s = slice(CUTS[i], CUTS[i + 1])
                V.tensor_single_scalar(deg[:, s], banks[7][:, s], 1.0, ALU.max).then_inc(deg_ready, 1)

            def norms(i, n, count, rows=True):
                s = slice(CUTS[i], CUTS[i + n])
                dve.wait_ge(root_ready, count)
                link(V.reciprocal(norm[:, s], root[:, s]))
                if rows:
                    V.tensor_tensor(scl[:, s], rstd[:, s], norm[:, s], ALU.mult)
                    V.tensor_tensor(off[:, s], nmr[:, s], norm[:, s], ALU.mult)
                V.tensor_copy(H[:, s, D:ROW], norm[:, s].unsqueeze(2).broadcast_to([P, CUTS[i + n] - CUTS[i], ROW - D])
                              ).then_inc(scale_ready, 1)

            def scale_rows(i, n):
                s = slice(CUTS[i], CUTS[i + 1])
                dve.wait_ge(pre_ready, n)
                V.tensor_tensor(H[:, s, 0:D], H[:, s, 0:D], norm[:, s].unsqueeze(2).broadcast_to([P, CUTS[i + 1] - CUTS[i], D]),
                                ALU.mult).then_inc(dve_rows, 1)

            link(statistics(6))
            dve.wait_ge(consts, 8)
            V.tensor_single_scalar(row_i[:, :], mask_i[:, :], 2, ALU.logical_shift_right)
            link(V.tensor_single_scalar(lane_b[:, :], mask_i[:, :], CB - 1, ALU.bitwise_and))
            V.tensor_tensor(diag[:, :], lane_b[:, :].broadcast_to([64, CB]), nodes_i[0:64, 0:CB], ALU.is_equal)
            V.tensor_tensor(pick[:, :], row_i[:, :].broadcast_to([64, 2 * P - DB]), pick_i[:, :], ALU.is_equal)
            rel_v = rel[:, :].rearrange("p (s j) -> p j s", j=SPC)
            first_v = first[:, :].rearrange("p (s j) -> p j s", j=SPC)
            for k in range(4):
                dve.wait_ge(dst_turned, k + 1)
                last = V.tensor_tensor(rel_v[:, 4 * k:4 * k + 4, :],
                                       banks[4 + k][:, 0:4 * STEPS].rearrange("p (j s) -> p j s", j=4),
                                       first_v[:, 4 * k:4 * k + 4, :], ALU.subtract)
            last.then_inc(rel_ready, 1)
            link(statistics(5))
            variances(0)
            dve.wait_ge(digits_ready, 1)
            V.memset(digit_a[P // 2:P, REAL_CH - 1:REAL_CH], float(DA))
            link(V.memset(digit_a[:, REAL_CH:CH], float(DA)))
            dve.wait_ge(cnt_clear, 1)
            hot_digits(0)
            scales(0)
            statistics(0)
            link(statistics(1))
            variances(1)
            cut_pass(0)
            cut_pass(1)
            hot_digits(1)
            scales(1)
            degrees(0)
            degrees(1)
            statistics(2)
            norms(0, 2, 1)
            link(statistics(3))
            variances(2)
            cut_pass(2)
            cut_pass(3)
            hot_digits(2)
            scales(2)
            degrees(2)
            degrees(3)
            link(statistics(4))
            variances(3)
            norms(2, 2, 2)
            dve.wait_ge(outside_ready, 1)
            link(V.tensor_tensor(outside[:, 2:3], outside[:, 0:1], outside[:, 1:2], ALU.add))
            V.memset(rel[P // 2:P, REAL_CH - 1:REAL_CH], FAR)
            V.memset(rel[:, REAL_CH:CH], FAR).then_inc(outside_summed, 1)
            scales(3)
            cut_pass(4)
            cut_pass(5)
            dve.wait_ge(outside_turned, 1)
            link(V.tensor_reduce(flag[0:1, 0:1], banks[6][0:1, 0:P], AX.X, ALU.max))
            V.tensor_single_scalar(flag_i[0:1, 0:1], flag[0:1, 0:1], 0.5, ALU.is_lt).then_inc(flag_ready, 1)
            hot_digits(3)
            degrees(4)
            degrees(5)
            norms(4, 2, 3)
            dve.wait_ge(scale_ready, 3)
            scale_rows(5, 2)
            cut_pass(6)
            degrees(6)
            norms(6, 1, 4, False)
            dve.wait_ge(scale_ready, 4)
            scale_rows(6, 1)

            quick = flag_value(dve)
            with dve.If(quick == 0):
                dve.sem_inc(own_general)
                V.tensor_tensor(n_i, rel[:, :], first[:, :], ALU.add).then_inc(own_general, 1)
                dve.wait_ge(own_general, 2)
                V.tensor_single_scalar(lo_i, n_i, P - 1, ALU.bitwise_and)
                V.tensor_single_scalar(hi_i, n_i, 7, ALU.arith_shift_right).then_inc(own_general, 1)
                dve.wait_ge(own_general, 3)
                V.tensor_copy(lo_f, lo_i)
                V.tensor_copy(hi_f, hi_i).then_inc(own_general, 1)
                dve.wait_ge(own_general, 4)
                with dve.Fori(0, GROUPS) as g:
                    dve.wait_ge(all_counted, g + 1)
                    for j in range(GC):
                        V.tensor_scalar(hot_lo[:, j, :], nodes[:, :], lo_f[:, bass.ds(g * GC + j, 1)], None, ALU.is_equal)
                        last = V.tensor_scalar(hot_hi[:, j, :], nodes[:, :], hi_f[:, bass.ds(g * GC + j, 1)], None, ALU.is_equal)
                    last.then_inc(all_hot_ready, 1)
                dve.wait_ge(all_counted, GROUPS + 1)
                V.tensor_copy(deg_sb[0:TILES, :], banks[4][0:TILES, 0:P]).then_inc(rows_counted, 1)
                dve.wait_ge(deg_turned, PASSES + 1)
                V.tensor_single_scalar(deg[:, :], banks[7][:, 0:TILES], 1.0, ALU.max).then_inc(all_norm, 1)
                dve.wait_ge(all_norm, 2)
                V.reciprocal(norm[:, :], root[:, :]).then_inc(all_norm, 1)
                dve.wait_ge(all_norm, 3)
                dve.wait_ge(table_done, 16 * BATCHES)
                V.tensor_tensor(scl[:, :], rstd[:, :], norm[:, :], ALU.mult)
                V.tensor_tensor(off[:, :], nmr[:, :], norm[:, :], ALU.mult)
                V.tensor_copy(H[:, :, D:ROW], norm[:, :].unsqueeze(2).broadcast_to([P, TILES, ROW - D])).then_inc(all_scaled, 1)

            V.tensor_copy(NODES[:, 0:WIN], nodes[:, :]).then_inc(bank_nodes, 1)
            dve.wait_ge(bank_nodes, 1)

            def finish(t):
                r = rows_of(t)
                dve.wait_ge(fin_mm, t + 1)
                dve.wait_ge(x_loaded, 16 * (t + 1))
                V.scalar_tensor_tensor(out=t1[0:r, :], in0=SELF[0:r, 0:D], scalar=FIN[0:r, D:D + 1], in1=x_st[0:r, :],
                                       op0=ALU.mult, op1=ALU.add).then_inc(t1_done, 1)
                dve.wait_ge(t1_done, t + 1)
                wait_prior(dve, stored, 16 * t)
                V.scalar_tensor_tensor(out=o_st[0:r, :], in0=FIN[0:r, 0:D], scalar=norm[0:r, bass.ds(t, 1)],
                                       in1=t1[0:r, :], op0=ALU.mult, op1=ALU.add).then_inc(out_ready, 1)

            with dve.If(quick == 1):
                def hots(i, half, k, prior):
                    for j in range(half * GC, half * GC + k):
                        if prior and j % 4 == 0:
                            dve.wait_ge(chunk_used, (i - 1) * SPC + j + 4)
                        V.tensor_scalar(OH[:, j, :], NODES[:, 0:WIN], rel[:, bass.ds(i * SPC + j, 1)], None,
                                        ALU.is_equal).then_inc(hot, 1)

                def add(g, half, k=GC, prior=True):
                    w = WIN + NPC * (k - 1)
                    at = g * (NPC * GC) + PAD - BACK
                    dve.wait_ge(chunk_used, g * GC + k)
                    if prior:
                        dve.wait_ge(group_added, g)
                    old = min(GW - NPC * GC, w) if prior else 0
                    for sums, ps in ((AG[:, :], agg_ps[half][:, :]),
                                     (SR[SP_ROW:SP_ROW + 1, :], s_ps[half][SP_ROW:SP_ROW + 1, :])):
                        if old:
                            last = V.tensor_tensor(sums[:, bass.ds(at, old)], sums[:, bass.ds(at, old)], ps[:, 0:old], ALU.add)
                        if w > old:
                            last = V.tensor_copy(sums[:, bass.ds(at + old, w - old)], ps[:, old:w])
                    last.then_inc(group_added, 1)

                def step(i, k, prior, last_add, fin):
                    hots(i, 0, min(k, GC), prior)
                    if last_add:
                        add(2 * i - 1, 1)
                    hots(i, 1, k - GC, prior)
                    if fin:
                        finish(i - 2)
                    add(2 * i, 0, GC, last_add)

                step(0, SPC, False, False, False)
                step(1, SPC, True, True, False)
                step(2, SPC, True, True, True)
                with dve.Fori(3, STEPS - 1) as i:
                    step(i, SPC, True, True, True)
                step(STEPS - 1, LAST_CH, True, True, True)
                add(GROUPS - 1, 1, LAST_CH - GC)
                finish(TILES - 2)
                finish(TILES - 1)
            with dve.Else():
                dve.wait_ge(sums_clear, 2)
                for primed in (all_hot, all_added, grel_ready):
                    dve.sem_inc(primed)
                with dve.Fori(0, GROUPS) as g:
                    dve.wait_ge(all_hot, g * TILES + 1)
                    dve.wait_ge(grel_ready, g * (TILES + 1) + 1)
                    V.tensor_tensor(grel[:, :], rel[:, bass.ds(g * GC, GC)], first[:, bass.ds(g * GC, GC)],
                                    ALU.add).then_inc(grel_ready, 1)
                    with dve.Fori(0, TILES) as w:
                        visit = g * TILES + w
                        dve.wait_ge(grel_ready, visit + g + 2)
                        dve.wait_ge(all_summed, visit + 1)
                        for j in range(GC):
                            last = V.tensor_scalar(OH[:, j, :], nodes[:, :], grel[:, j:j + 1], None, ALU.is_equal)
                        last.then_inc(all_hot, 1)
                        dve.wait_ge(all_hot, visit + 2)
                        V.tensor_single_scalar(grel[:, :], grel[:, :], -float(P), ALU.add).then_inc(grel_ready, 1)
                        dve.wait_ge(all_summed, visit + 2)
                        dve.wait_ge(all_added, visit + 1)
                        at = w * P + PAD
                        V.tensor_tensor(AG[:, bass.ds(at, P)], AG[:, bass.ds(at, P)], AGG_A[:, 0:P], ALU.add)
                        V.tensor_tensor(SR[SP_ROW:SP_ROW + 1, bass.ds(at, P)], SR[SP_ROW:SP_ROW + 1, bass.ds(at, P)],
                                        S_A[SP_ROW:SP_ROW + 1, 0:P], ALU.add).then_inc(all_added, 1)
                finish(0)
                with dve.Fori(1, TILES - 1) as t:
                    finish(t)
                finish(TILES - 1)

        @block.tensor
        def _(pe):
            T = nc.tensor
            for k in range(2 * SPC):
                raw = (b_raw, a_raw)[k // SPC]
                if k % SPC == 0:
                    pe.wait_ge(digits_float, k // SPC + 1)
                j = k % 8
                last = T.transpose(banks[k // 8][:, :].bitcast(bf16)[:, j * STEPS:(j + 1) * STEPS],
                                   raw[:, (k % SPC) * P:(k % SPC + 1) * P], ident_b[0:STEPS, 0:STEPS])
                if j == 7:
                    last.then_inc(digits_turned, 1)
            pe.wait_ge(dst_float, 1)
            for k in range(SPC):
                last = T.transpose(banks[4 + k // 4][:, (k % 4) * STEPS:(k % 4 + 1) * STEPS], dst_f[:, k * P:(k + 1) * P],
                                   ident[0:STEPS, 0:STEPS])
                if k % 4 == 3:
                    last.then_inc(dst_turned, 1)

            def count_passes(n):
                pe.wait_ge(hot_ready, n + 1)
                for i in range(*HOT_PASSES[n]):
                    m0 = (i - HOT_PASSES[n][0]) * PC // CB
                    for m in range(PC // CB):
                        q0 = (m * CB // GC) * 4
                        last = T.matmul(banks[4 + i % 2][0:64, q0 * CB:(q0 + DA) * CB],
                                        hot_b[:, m0 + m].rearrange("p v c -> p (v c)"),
                                        hot_a[:, m0 + m].rearrange("p v c -> p (v c)"),
                                        start=(m == 0), stop=(m == PC // CB - 1), skip_group_check=True)
                    last.then_inc(counted, 1)

            def turn_counts(i):
                t0, t1 = CUTS[i], CUTS[i + 1]
                pe.wait_ge(cnt_added, i + 1)
                if i:
                    pe.wait_ge(deg_ready, i)
                for a in range(TQ):
                    q0 = PAD // DB + t0 * TQ + a
                    last = T.matmul(banks[7][:, t0:t1], pick[:, P - DB - DB * a:2 * P - DB - DB * a],
                                    cnt[:, q0:q0 + (t1 - t0 - 1) * TQ + 1:TQ],
                                    start=(a == 0), stop=(a == TQ - 1), skip_group_check=True)
                last.then_inc(deg_turned, 1)

            pe.wait_ge(digits_ready, 1)
            pe.wait_ge(src_float, 1)
            for k in range(SPC):
                last = T.transpose(banks[k // 4][:, (k % 4) * STEPS:(k % 4 + 1) * STEPS],
                                   src_f[:, k * P:(k + 1) * P], ident[0:STEPS, 0:STEPS])
                if k % 4 == 3:
                    last.then_inc(src_turned, 1)
            count_passes(0)
            turn_counts(0)
            turn_counts(1)
            count_passes(1)
            turn_counts(2)
            turn_counts(3)
            count_passes(2)
            pe.wait_ge(outside_summed, 1)
            T.transpose(banks[6][0:1, 0:P], outside[:, 2:3], ident[:, :]).then_inc(outside_turned, 1)
            turn_counts(4)
            turn_counts(5)
            pe.wait_ge(flag_ready, 1)
            pe.wait_ge(w_loaded, 32)
            for k in range(2):
                last = T.transpose(banks[6][:, k * D:(k + 1) * D], w_in[:, k * D:(k + 1) * D], ident[:, :])
            last.then_inc(w_turned, 1)
            count_passes(3)
            turn_counts(6)

            quick = flag_value(pe)
            with pe.If(quick == 0):
                pe.sem_inc(all_counted)

                def count_group(g, start):
                    pe.wait_ge(all_hot_ready, g + 1)
                    for j in range(GC):
                        last = T.matmul(banks[4][:, 0:P], hot_hi[:, j, :], hot_lo[:, j, :],
                                        start=start and j == 0, stop=False, skip_group_check=True)
                    last.then_inc(all_counted, 1)

                count_group(0, True)
                with pe.Fori(1, GROUPS) as g:
                    count_group(g, False)
                pe.wait_ge(rows_counted, 1)
                T.transpose(banks[7][:, 0:TILES], deg_sb[0:TILES, :], ident[0:TILES, 0:TILES]).then_inc(deg_turned, 1)

            def turn_tile(t):
                r = rows_of(t)
                pe.wait_ge(h_loaded, 16 * (t + 1))
                T.transpose(TURN[:, 0:r], h_st[0:r, 0:D], ident[0:r, 0:r]).then_inc(h_turned, 1)

            def finish_tile(t):
                r = rows_of(t)
                pe.wait_ge(hT_ready, t + 1)
                pe.wait_ge(staged, t + 1)
                wait_prior(pe, out_ready, t)
                T.matmul(SELF[0:r, 0:D], hT[:, 0:r], wT[:, 0:D], start=True, stop=True)
                T.matmul(FIN[0:r, 0:D + 1], s_st[0:1, 0:r], brow[0:1, :], start=True, stop=False, skip_group_check=True)
                T.matmul(FIN[0:r, 0:D], a_st[:, 0:r], wT[:, D:2 * D], start=False, stop=True,
                         skip_group_check=True).then_inc(fin_mm, 1)

            def sum_chunk(agg, s_out, j, start, stop):
                T.matmul(agg, G[:, j, 0:D], OH[:, j, :], start=start, stop=stop, skip_group_check=True)
                return T.matmul(s_out, G[:, j, D - SP_ROW:D + 1], OH[:, j, :], start=start, stop=stop, skip_group_check=True)

            pe.wait_ge(w_ready, 1)
            with pe.If(quick == 1):
                def step(i, k, turn, adds):
                    for j in range(k):
                        half, jj = j // GC, j % GC
                        if jj == 0 and adds:
                            pe.wait_ge(group_added, 2 * i - 1 + half)
                        pe.wait_ge(landed[j], 16 * (i + 1))
                        pe.wait_ge(hot, i * SPC + j + 1)
                        c0 = NPC * jj
                        stop = jj == GC - 1 or j == k - 1
                        last = sum_chunk(agg_ps[half][:, c0:c0 + WIN],
                                         s_ps[half][0:SP_ROW + 1, c0:c0 + WIN], j, jj == 0, stop)
                        last.then_inc(chunk_used, 1)
                        if turn and j == 0:
                            turn_tile(i - 2)
                        if turn and j == 3:
                            finish_tile(i - 2)

                step(0, SPC, False, False)
                step(1, SPC, False, True)
                step(2, SPC, True, True)
                with pe.Fori(3, STEPS - 1) as i:
                    step(i, SPC, True, True)
                step(STEPS - 1, LAST_CH, True, True)
                for t in (TILES - 2, TILES - 1):
                    turn_tile(t)
                    finish_tile(t)
            with pe.Else():
                pe.sem_inc(all_summed)
                with pe.Fori(0, GROUPS) as g:
                    for j in range(GC):
                        pe.wait_ge(landed[j], 16 * (g + 1))
                    pe.sem_inc(waited)
                    with pe.Fori(0, TILES) as w:
                        visit = g * TILES + w
                        pe.wait_ge(all_added, visit + 1)
                        pe.wait_ge(all_hot, visit + 2)
                        for j in range(GC):
                            last = sum_chunk(AGG_A[:, 0:P], S_A[0:SP_ROW + 1, 0:P], j, j == 0, j == GC - 1)
                        last.then_inc(all_summed, 1)
                turn_tile(0)
                finish_tile(0)
                with pe.Fori(1, TILES - 1) as t:
                    turn_tile(t)
                    finish_tile(t)
                turn_tile(TILES - 1)
                finish_tile(TILES - 1)


def kernel(x, src, dst, L0_gnn_W, L0_gnn_b):
    import numpy as np
    import concourse.bacc as bacc
    from concourse.bass_utils import run_bass_kernel_spmd

    nc = bacc.Bacc("TRN2", target_bir_lowering=False, num_devices=1)
    arrays, args = {}, []
    for name, a in (("x", x), ("src", src), ("dst", dst), ("W", L0_gnn_W), ("b", L0_gnn_b)):
        a = np.ascontiguousarray(a)
        arrays[f"in_{name}"] = a
        args.append(nc.dram_tensor(f"in_{name}", a.shape, mybir.dt.from_np(a.dtype), kind="ExternalInput").ap())
    out = nc.dram_tensor("out_nodes", args[0].shape, mybir.dt.float32, kind="ExternalOutput").ap()
    gnn_layer(nc, *args, out)
    r = run_bass_kernel_spmd(nc, [arrays], core_ids=[0])
    return r.results[0]["out_nodes"]
```

```python
import concourse.bass as bass
from concourse import mybir
from contextlib import ExitStack


def gnn_layer(nc, x, src, dst, W, b, out):
    f32, bf16, i32 = mybir.dt.float32, mybir.dt.bfloat16, mybir.dt.int32
    ALU = mybir.AluOpType
    ACT = mybir.ActivationFunctionType
    AX = mybir.AxisListType

    N, D = x.shape
    E = src.shape[0]
    P = 128
    TILES = -(-N // P)
    LAST_ROWS = N - (TILES - 1) * P
    SPC = 16
    STEP_E = SPC * P
    STEPS = -(-E // STEP_E)
    CH = STEPS * SPC
    REAL_CH = -(-E // P)
    LAST_CH = REAL_CH - (STEPS - 1) * SPC
    FULL_ROWS = E // STEP_E
    LIST_LOADS = 48 if FULL_ROWS >= 16 else 32
    TAIL_E = E - FULL_ROWS * STEP_E
    NPC = N * P // E
    GC = 8
    GROUPS = CH // GC
    WIN = P
    BACK = (WIN - NPC) // 2
    GW = WIN + NPC * (GC - 1)
    PAD = P // 2
    COLS = TILES * P + 2 * PAD
    ROW = D + 4
    EPS = 1e-5
    FAR = -32768.0
    BATCHES = 7
    PASSES = 7
    CUTS = [0] + [TILES // PASSES * (i + 1) - 1 for i in range(PASSES - 1)] + [TILES]
    ORDER = [6, 5, 0, 1, 2, 3, 4]
    STAT_GROUPS = [(CUTS[5], CUTS[7]), (CUTS[0], CUTS[2]), (CUTS[2], CUTS[4]), (CUTS[4], CUTS[5])]
    DB, DA = 16, 12
    CB = 4
    PC = CH // PASSES
    PW = (PC // GC - 1) * 4 + DA
    HOT_PASSES = [(0, 2), (2, 4), (4, 6), (6, 7)]
    HPC = 2 * PC
    Q = COLS // DB
    ES = 6 if STEPS > 40 else 1
    EC, EG = ES * SPC, ES * SPC // GC
    ET = -(-((EG - 1) * NPC * GC - BACK + GW) // P)
    LATE = ES + EG + 2
    assert ET == ES + 1 and LATE + ET < STEPS - 1
    BOUNDS = [ES, ES + 1, ES + 2, ES + 3] + ([ES + EG - 1, ES + EG] if ES > 1 else []) + [ES + EG + 1, LATE, LATE + ET, STEPS - 1, STEPS]
    BOUNDS = sorted(set(BOUNDS))
    TQ = P // DB
    assert D == P and NPC == 8 and STEPS == TILES and TILES % PASSES == 0 and CH == PASSES * PC
    assert E % P == P // 2 and PAD % DB == 0
    assert PAD + TILES * P <= COLS and (GROUPS - 1) * NPC * GC + PAD - BACK + GW <= COLS

    row_of = lambda a, t, k: a[t * P:(t + k) * P, :].rearrange("(t p) d -> p t d", p=P)

    table = nc.dram_tensor("table", (TILES * P, ROW), f32, kind="Internal").ap()

    ctx = ExitStack()
    with ctx:
        sb = lambda name, shape, dt: ctx.enter_context(nc.sbuf_tensor(name, shape, dt))
        sem = lambda name: ctx.enter_context(nc.semaphore(name))
        banks = [ctx.enter_context(nc.psum_tensor(f"bank{i}", [P, 512], f32)) for i in range(8)]

        AG = sb("AG", [P, max(COLS, TILES * ROW)], f32)
        SR = sb("SR", [P, COLS], f32)
        EX = sb("EX", [P, EC * ROW], f32)
        xrows = AG[:, 0:TILES * ROW].rearrange("p (t r) -> p t r", r=ROW)
        xall, H = xrows[:, :, 0:D], xrows
        ER = EX[:, :].rearrange("p (j r) -> p j r", r=ROW)
        SP_ROW = 96
        GO = sb("GO", [P, SPC * (ROW + WIN)], f32)
        raw0 = EC * ROW - 3 * STEP_E
        FREE = raw0 // ROW
        src_raw, src_f, digits_raw = (EX[0:STEPS, raw0 + i * STEP_E:raw0 + (i + 1) * STEP_E] for i in range(3))
        dst_raw, dst_f = (GO[0:STEPS, i * STEP_E:(i + 1) * STEP_E] for i in range(2))
        dst_raw, src_raw = dst_raw.bitcast(i32), src_raw.bitcast(i32)
        b_raw = digits_raw[:, 0:STEP_E // 2].bitcast(bf16)
        a_raw = digits_raw[:, STEP_E // 2:STEP_E].bitcast(bf16)
        rel = sb("rel", [P, CH], f32)
        srci = sb("srci", [P, CH], i32)
        first = sb("first", [P, CH], i32)
        a_first = sb("a_first", [P, 2], f32)
        a_first_i = sb("a_first_i", [P, 2], i32)
        ident_b = sb("ident_b", [P, P], bf16)
        nodes = sb("nodes", [P, WIN], f32)
        nodes_i = sb("nodes_i", [P, WIN], i32)
        ident = sb("ident", [P, P], f32)
        w_in = sb("w_in", [P, 2 * D], f32)
        wT = sb("wT", [P, 2 * D], f32)
        brow = sb("brow", [1, D + 1], f32)
        stats = sb("stats", [P, TILES, 6], f32)
        mean2 = sb("mean2", [P, TILES], f32)
        dif = sb("dif", [P, TILES], f32)
        var = sb("var", [P, TILES], f32)
        std = sb("std", [P, TILES], f32)
        rstd = sb("rstd", [P, TILES], f32)
        nmr = sb("nmr", [P, TILES], f32)
        scl = sb("scl", [P, TILES], f32)
        off = sb("off", [P, TILES], f32)
        edge_of_window = sb("edge_of_window", [P, 1], f32)
        outside = sb("outside", [P, 3], f32)
        flag = sb("flag", [1, 2], f32)
        flag_i = sb("flag_i", [1, 1], i32)
        place_i = sb("place_i", [P, 1], i32)
        place = sb("place", [P, 1], f32)
        lane_b = sb("lane_b", [64, 1], i32)
        diag = sb("diag", [64, CB], f32)
        pick = sb("pick", [64, 2 * P - DB], f32)
        step_node = sb("step_node", [P, STEPS], f32)
        chunk_node = sb("chunk_node", [P, SPC], f32)
        row_i = sb("row_i", [64, 1], i32)
        counting = sb("counting", [P, Q + PW * (CB + 1)], f32)
        cnt = counting[0:64, 0:Q]
        part = counting[0:64, Q:Q + PW]
        own = counting[0:64, Q + PW:Q + PW * (CB + 1)].rearrange("p (q c) -> p q c", c=CB)
        deg_sb = sb("deg_sb", [P, P], f32)
        deg = sb("deg", [P, TILES], f32)
        root = sb("root", [P, TILES], f32)
        norm = sb("norm", [P, TILES], f32)
        idx = sb("idx", [P, SPC], i32)
        G = GO[:, 0:SPC * ROW].rearrange("p (j r) -> p j r", r=ROW)
        OH = GO[:, SPC * ROW:SPC * (ROW + WIN)].rearrange("p (j n) -> p j n", n=WIN)
        waste = GO[:, 0:CH // 2].bitcast(bf16)
        h_st = sb("h_st", [P, ROW], f32)
        x_st = sb("x_st", [P, D], f32)
        a_st = sb("a_st", [P, P], f32)
        s_st = sb("s_st", [1, P], f32)
        hT = sb("hT", [P, P], f32)
        t1 = sb("t1", [P, D], f32)
        o_st = sb("o_st", [P, D], f32)
        grel = sb("grel", [P, GC], f32)
        x_last, o_last = w_in[:, 0:D], w_in[:, D:2 * D]
        early_raw, early_f = a_st[0:EC, :].bitcast(i32), hT[0:EC, :]
        early_idx = sb("early_idx", [P, EC], i32)
        tile_i = x_st[:, 0:EC].bitcast(i32)
        tile_f = deg_sb[:, 0:EC]
        wide = first[:, 0:GC * P]
        at_place = wide.bitcast(f32)
        early_oh = counting[:, 0:GC * WIN].rearrange("p (j n) -> p j n", n=WIN)
        found = stats[:, :, :].rearrange("p t k -> p (t k)")[:, 0:GC // 2 * TILES].rearrange("p (j t) -> p j t", t=TILES)
        e_stats = sb("e_stats", [P, GC, 6], f32)
        e_mean2, e_dif, e_var, e_std, e_rstd, e_norm, e_scl, e_off = (
            sb(f"e_{name}", [P, GC], f32) for name in ("mean2", "dif", "var", "std", "rstd", "norm", "scl", "off"))

        scr = SR[:, :]
        digit_b = scr[:, 0:CH // 2].bitcast(bf16)
        digit_a = scr[:, CH // 2:CH].bitcast(bf16)
        hot_b = scr[:, CH:CH + DB * HPC // 2].bitcast(bf16).rearrange("p (m v c) -> p m v c", m=HPC // CB, c=CB)
        o0 = CH + DB * HPC // 2
        hot_a = scr[:, o0:o0 + DA * HPC // 2].bitcast(bf16).rearrange("p (m v c) -> p m v c", m=HPC // CB, c=CB)
        o0 += DA * HPC // 2
        b_i, a_i = (scr[0:STEPS, o0 + i * STEP_E:o0 + (i + 1) * STEP_E].bitcast(i32) for i in range(2))
        n_i, lo_i, hi_i = (scr[:, i * CH:(i + 1) * CH].bitcast(i32) for i in range(3))
        lo_f, hi_f = (scr[:, i * CH:(i + 1) * CH] for i in range(3, 5))
        o1 = 5 * CH
        hot_lo = scr[:, o1:o1 + GC * P // 2].bitcast(bf16).rearrange("p (j n) -> p j n", j=GC)
        hot_hi = scr[:, o1 + GC * P // 2:o1 + GC * P].bitcast(bf16).rearrange("p (j n) -> p j n", j=GC)

        dst_in = sem("dst_in")
        src_in = sem("src_in")
        x_in = [sem(f"x_in{i}") for i in range(BATCHES)]
        w_loaded = sem("w_loaded")
        edge_pads = sem("edge_pads")
        consts = sem("consts")
        pool_step = sem("pool_step")
        outside_summed = sem("outside_summed")
        own_general = sem("own_general")
        dve_step = sem("dve_step")
        act_step = sem("act_step")
        dst_float = sem("dst_float")
        src_float = sem("src_float")
        w_turned = sem("w_turned")
        w_ready = sem("w_ready")
        dst_turned = sem("dst_turned")
        src_turned = sem("src_turned")
        src_ready = sem("src_ready")
        flag_ready = sem("flag_ready")
        b_split = sem("b_split")
        a_split = sem("a_split")
        digits_float = sem("digits_float")
        digits_turned = sem("digits_turned")
        digits_ready = sem("digits_ready")
        rel_ready = sem("rel_ready")
        outside_ready = sem("outside_ready")
        outside_turned = sem("outside_turned")
        deg_turned = sem("deg_turned")
        rows_counted = sem("rows_counted")
        bank_nodes = sem("bank_nodes")
        hot_ready = sem("hot_ready")
        counted = sem("counted")
        cnt_added = sem("cnt_added")
        grel_ready = sem("grel_ready")
        all_hot = sem("all_hot")
        all_summed = sem("all_summed")
        all_added = sem("all_added")
        all_counted = sem("all_counted")
        all_hot_ready = sem("all_hot_ready")
        deg_ready = sem("deg_ready")
        pre_ready = sem("pre_ready")
        scale_ready = sem("scale_ready")
        act_rows = sem("act_rows")
        dve_rows = sem("dve_rows")
        all_norm = sem("all_norm")
        all_scaled = sem("all_scaled")
        all_rows = sem("all_rows")
        table_again = sem("table_again")
        tile_again = sem("tile_again")
        x_again = sem("x_again")
        early_in = sem("early_in")
        early_float = sem("early_float")
        early_turned = sem("early_turned")
        early_ready = sem("early_ready")
        early_tiles = sem("early_tiles")
        early_landed = sem("early_landed")
        wide_in = sem("wide_in")
        early_step = sem("early_step")
        place_ready = sem("place_ready")
        looked_up = sem("looked_up")
        picked = sem("picked")
        e_var_ready = sem("e_var_ready")
        e_std_ready = sem("e_std_ready")
        e_scaled = sem("e_scaled")
        e_scl_ready = sem("e_scl_ready")
        e_rows = sem("e_rows")
        e_hot = sem("e_hot")
        e_used = sem("e_used")
        e_added = sem("e_added")
        consts_float = sem("consts_float")
        root_ready = sem("root_ready")
        var_ready = sem("var_ready")
        std_ready = sem("std_ready")
        ln_ready = sem("ln_ready")
        table_done = sem("table_done")
        sums_clear = sem("sums_clear")
        idx_ready = sem("idx_ready")
        waited = sem("waited")
        landed = [sem(f"landed{i}") for i in range(SPC)]
        hot = sem("hot")
        chunk_used = sem("chunk_used")
        group_added = sem("group_added")
        h_loaded = sem("h_loaded")
        x_loaded = sem("x_loaded")
        x_last_in = sem("x_last_in")
        h_turned = sem("h_turned")
        hT_ready = sem("hT_ready")
        staged = sem("staged")
        fin_mm = sem("fin_mm")
        t1_done = sem("t1_done")
        out_ready = sem("out_ready")
        stored = sem("stored")

        SUM_A, SUM_B, SUM_E, LOOK, TURN, SELF, FIN, NODES = banks
        agg_ps = [SUM_A, SUM_B, SUM_E]
        s_ps = [bank[:, 256:512] for bank in agg_ps]
        DEG = [banks[7], banks[2]]

        def wait_prior(eng, what, value):
            if not (isinstance(value, int) and value == 0):
                eng.wait_ge(what, value)

        def walk(eng, step):
            for start, end in zip(BOUNDS, BOUNDS[1:]):
                if end - start == 1:
                    step(start, start)
                else:
                    with eng.Fori(start, end) as i:
                        step(i, start)

        look_group = lambda i, a: i - ES if a < ES + EG else None
        sum_group = lambda i, a: i - ES - 1 if ES < a <= ES + EG else None
        add_group = lambda i, a: i - ES - 2 if ES + 2 <= a < LATE else None
        done_tile = lambda i, a: i - 2 if a - 2 >= ET else None
        late_tile = lambda i, a: i - LATE if LATE <= a < LATE + ET else None

        def order(i, a):
            if a < LATE:
                return i - 2 - ET
            return LATE - 2 - ET + 2 * (i - LATE) if a < LATE + ET else i - 2

        def next_order(i, a):
            return order(i, a) + (2 if late_tile(i, a) is not None else 1)

        is_last = lambda t: isinstance(t, int) and t == TILES - 1

        def rows_of(t):
            return LAST_ROWS if is_last(t) else P

        def flag_value(eng):
            eng.wait_ge(flag_ready, 1)
            return eng.value_load(flag_i[0:1, 0:1], min_val=0, max_val=1)

        block = ctx.enter_context(nc.Block())

        @block.sync
        def _(sp):
            def load_list(raw, lst, list_in, pads):
                k = FULL_ROWS // 16 * 16
                if k:
                    sp.dma_start(raw[0:k, :], lst[0:k * STEP_E].rearrange("(s e) -> s e", e=STEP_E)).then_inc(list_in, 16)
                sp.wait_ge(edge_pads, pads)
                sp.dma_start(raw[k:FULL_ROWS, :], lst[k * STEP_E:FULL_ROWS * STEP_E].rearrange("(s e) -> s e", e=STEP_E)).then_inc(list_in, 16)
                sp.dma_start(raw[FULL_ROWS:STEPS, 0:TAIL_E], lst[FULL_ROWS * STEP_E:E].rearrange("(s e) -> s e", s=1)).then_inc(list_in, 16)

            sp.dma_start(early_raw, src[0:EC * P].rearrange("(c e) -> c e", e=P)).then_inc(early_in, 16)
            load_list(dst_raw, dst, dst_in, 1)
            for i in ORDER:
                t0, t1 = CUTS[i], min(CUTS[i + 1], TILES - 1)
                sp.dma_start(xall[:, t0:t1, :], row_of(x, t0, t1 - t0)).then_inc(x_in[i], 16)
                if t1 == TILES - 1:
                    sp.wait_ge(consts, 2)
                    sp.dma_start(xall[0:LAST_ROWS, TILES - 1, :], x[(TILES - 1) * P:N, :]).then_inc(x_in[i], 16)
                if i == 6:
                    load_list(src_raw, src, src_in, 2)
            sp.dma_start(w_in[:, :], W).then_inc(w_loaded, 16)
            sp.dma_start(brow[0:1, 0:D], b.rearrange("(a d) -> a d", a=1)).then_inc(w_loaded, 16)

            for i, rows, n in ((0, act_rows, 1), (1, act_rows, 2), (2, act_rows, 3), (3, act_rows, 4),
                               (5, dve_rows, 1), (4, act_rows, 5), (6, dve_rows, 2)):
                sp.wait_ge(rows, n)
                sp.dma_start(row_of(table, CUTS[i], CUTS[i + 1] - CUTS[i]), H[:, CUTS[i]:CUTS[i + 1], :]).then_inc(table_done, 16)
            sp.wait_ge(table_done, 16 * BATCHES)
            quick = flag_value(sp)
            with sp.If(quick == 0):
                sp.dma_start(xall[:, 0:TILES - 1, :], row_of(x, 0, TILES - 1)).then_inc(x_again, 16)
                sp.dma_start(xall[0:LAST_ROWS, TILES - 1, :], x[(TILES - 1) * P:N, :]).then_inc(x_again, 16)
                sp.wait_ge(all_rows, 1)
                sp.dma_start(row_of(table, 0, TILES), H).then_inc(table_again, 16)
                sp.wait_ge(table_again, 16)

            def load_rows(t, n):
                r = rows_of(t)
                wait_prior(sp, h_turned, n)
                sp.dma_start(h_st[0:r, :], table[bass.ds(t * P, r), :]).then_inc(h_loaded, 16)
                if is_last(t):
                    sp.wait_ge(w_turned, 1)
                else:
                    wait_prior(sp, t1_done, n)
                sp.dma_start((x_last if is_last(t) else x_st)[0:r, :], x[bass.ds(t * P, r), :]).then_inc(
                    x_last_in if is_last(t) else x_loaded, 16)

            def store_rows(t, n):
                r = rows_of(t)
                sp.wait_ge(out_ready, n + 1)
                sp.dma_start(out[bass.ds(t * P, r), :], (o_last if is_last(t) else o_st)[0:r, :]).then_inc(stored, 16)

            def step(i, a):
                t, late = done_tile(i, a), late_tile(i, a)
                if t is None:
                    return
                n = order(i, a)
                if late is not None:
                    load_rows(late, n + 1)
                    store_rows(t, n)
                    load_rows(i - 1, n + 2)
                    store_rows(late, n + 1)
                else:
                    load_rows(i - 1, n + 1)
                    store_rows(t, n)

            with sp.If(quick == 1):
                load_rows(ET, 0)
                walk(sp, step)
                load_rows(TILES - 1, TILES - 1)
                store_rows(TILES - 2, TILES - 2)
                store_rows(TILES - 1, TILES - 1)
            with sp.Else():
                load_rows(0, 0)
                with sp.Fori(0, TILES - 2) as t:
                    load_rows(t + 1, t + 1)
                    store_rows(t, t)
                load_rows(TILES - 1, TILES - 1)
                store_rows(TILES - 2, TILES - 2)
                store_rows(TILES - 1, TILES - 1)
            sp.wait_ge(stored, 16 * TILES)

        @block.gpsimd
        def _(pool):
            pool.memset(ident[:, :], 0.0).then_inc(pool_step, 1)
            pool.wait_ge(pool_step, 1)
            pool.affine_select(out=ident[:, :], in_=ident[:, :], compare_op=ALU.not_equal, fill=1.0, base=0,
                               pattern=[[-1, P]], channel_multiplier=1).then_inc(consts, 1)
            pool.memset(xall[:, TILES - 1, :], 0.0).then_inc(consts, 1)
            pool.iota(a_first_i[:, :], pattern=[[-NPC * GC // DB, 2]], base=PAD // DB,
                      channel_multiplier=-2 * NPC * GC // DB).then_inc(consts, 1)
            pool.iota(nodes_i[:, :], pattern=[[1, WIN]], base=0, channel_multiplier=0).then_inc(consts, 1)
            pool.iota(place_i[:, :], pattern=[[0, 1]], base=0, channel_multiplier=1).then_inc(consts, 1)
            pool.memset(brow[0:1, D:D + 1], 1.0).then_inc(consts, 1)

            pool.wait_ge(early_ready, 1)
            for c in range(EC):
                if c == FREE:
                    pool.wait_ge(src_turned, 4)
                    pool.wait_ge(digits_turned, 4)
                    pool.sem_inc(waited)
                pool.indirect_dma_start(ER[:, c, 0:D], None, x[:, :],
                                        bass.IndirectOffsetOnAxis(ap=early_idx[:, c:c + 1], axis=0)).then_inc(early_landed, 16)

            quick = flag_value(pool)
            pool.wait_ge(table_done, 16 * BATCHES)

            def gather(j):
                pool.indirect_dma_start(G[:, j, :], None, table[:, :],
                                        bass.IndirectOffsetOnAxis(ap=idx[:, j:j + 1], axis=0)).then_inc(landed[j], 16)

            with pool.If(quick == 1):
                def step(i, a):
                    for j in range(LAST_CH if a == STEPS - 1 else SPC):
                        if j % GC == 0:
                            pool.wait_ge(idx_ready, 2 * (i - ES) + j // GC + 1)
                            pool.sem_inc(waited)
                        if a > ES and j % 4 == 0:
                            pool.wait_ge(chunk_used, (i - ES - 1) * SPC + j + 4)
                            pool.sem_inc(waited)
                        gather(j)

                walk(pool, step)
            with pool.Else():
                pool.wait_ge(table_again, 16)
                pool.wait_ge(all_rows, 1)
                pool.memset(AG[:, :], 0.0).then_inc(sums_clear, 1)
                pool.wait_ge(sums_clear, 1)
                pool.memset(SR[SP_ROW:SP_ROW + 1, :], 0.0).then_inc(sums_clear, 1)
                with pool.Fori(0, GROUPS) as g:
                    pool.wait_ge(idx_ready, g + 1)
                    pool.wait_ge(all_summed, g * TILES + 1)
                    pool.sem_inc(waited)
                    for j in range(GC):
                        gather(j)

        @block.scalar
        def _(act):
            act.wait_ge(early_turned, 1)
            nc.scalar.copy(early_idx[:, :], banks[7][:, 0:EC]).then_inc(early_ready, 1)
            act.wait_ge(b_split, 1)
            nc.scalar.copy(b_raw, b_i).then_inc(digits_float, 1)
            act.wait_ge(a_split, 1)
            act.wait_ge(consts_float, 1)
            for half in range(2):
                h = slice(half * STEP_E // 2, (half + 1) * STEP_E // 2)
                last = nc.scalar.activation(a_raw[:, h], a_i[:, h], ACT.Identity, bias=a_first[0:STEPS, half:half + 1])
            last.then_inc(digits_float, 1)
            for k in range(4):
                act.wait_ge(digits_turned, k + 1)
                digit = (digit_b, digit_a)[k // 2]
                last = nc.scalar.copy(digit.rearrange("p (s j) -> p j s", j=SPC)[:, 8 * (k % 2):8 * (k % 2) + 8, :],
                                      banks[k][:, :].bitcast(bf16)[:, 0:8 * STEPS].rearrange("p (j s) -> p j s", j=8))
            last.then_inc(digits_ready, 1)

            act.wait_ge(dst_in, LIST_LOADS)
            nc.scalar.copy(dst_f, dst_raw).then_inc(dst_float, 1)
            act.wait_ge(src_in, LIST_LOADS)
            nc.scalar.copy(src_f, src_raw).then_inc(src_float, 1)

            def deviations(g):
                s = slice(*STAT_GROUPS[g])
                act.wait_ge(var_ready, g + 1)
                nc.scalar.activation(std[:, s], var[:, s], ACT.Sqrt).then_inc(std_ready, 1)

            def roots(i, n):
                s = slice(CUTS[i], CUTS[i + n])
                act.wait_ge(deg_ready, i + n)
                nc.scalar.activation(root[:, s], deg[:, s], ACT.Sqrt).then_inc(root_ready, 1)

            def normalize(i, scale, offset, ready):
                for t in range(CUTS[i], CUTS[i + 1]):
                    last = nc.scalar.activation(H[:, t, 0:D], xall[:, t, :], ACT.Relu,
                                                scale=scale[:, t:t + 1], bias=offset[:, t:t + 1])
                last.then_inc(ready, 1)

            for k in range(4):
                act.wait_ge(src_turned, k + 1)
                last = nc.scalar.copy(
                    srci[:, :].rearrange("p (s j) -> p j s", j=SPC)[:, 4 * k:4 * k + 4, :],
                    banks[k][:, 0:4 * STEPS].rearrange("p (j s) -> p j s", j=4))
            last.then_inc(src_ready, 1)
            deviations(0)
            act.wait_ge(rel_ready, 1)
            nc.scalar.activation(waste, rel[:, :], ACT.Relu, bias=edge_of_window[:, :],
                                 accum_out=outside[:, 0:1]).then_inc(act_step, 1)
            act.wait_ge(act_step, 1)
            nc.scalar.activation(waste, rel[:, :], ACT.Relu, scale=-1.0,
                                 accum_out=outside[:, 1:2]).then_inc(outside_ready, 1)
            act.wait_ge(ln_ready, 1)
            normalize(6, rstd, nmr, pre_ready)
            deviations(1)
            normalize(5, rstd, nmr, pre_ready)
            roots(0, 2)
            deviations(2)
            act.wait_ge(scale_ready, 1)
            normalize(0, scl, off, act_rows)
            normalize(1, scl, off, act_rows)
            roots(2, 2)
            deviations(3)
            act.wait_ge(scale_ready, 2)
            normalize(2, scl, off, act_rows)
            normalize(3, scl, off, act_rows)
            act.wait_ge(w_turned, 1)
            nc.scalar.copy(wT[:, :], banks[6][:, 0:2 * D]).then_inc(w_ready, 1)
            roots(4, 2)
            act.wait_ge(scale_ready, 3)
            normalize(4, scl, off, act_rows)
            roots(6, 1)

            quick = flag_value(act)
            act.wait_ge(src_ready, 1)

            def hand_idx(i, half):
                nc.scalar.copy(idx[:, half * GC:(half + 1) * GC],
                               srci[:, bass.ds(i * SPC + half * GC, GC)]).then_inc(idx_ready, 1)

            def turned_h(t, n):
                r = rows_of(t)
                act.wait_ge(h_turned, n + 1)
                nc.scalar.copy(hT[:, 0:r], TURN[:, 0:r]).then_inc(hT_ready, 1)

            def stage(t, n, adds, added=group_added):
                act.wait_ge(added, adds)
                wait_prior(act, fin_mm, n)
                nc.scalar.copy(a_st[:, :], AG[:, bass.ds(t * P + PAD, P)])
                nc.scalar.copy(s_st[:, :], SR[SP_ROW:SP_ROW + 1, bass.ds(t * P + PAD, P)]).then_inc(staged, 1)

            with act.If(quick == 1):
                def load_wide(e):
                    act.dma_start(wide, src[bass.ds(e * GC * P, GC * P)].rearrange("(o e) -> o e", o=1)
                                  .broadcast_to([P, GC * P])).then_inc(wide_in, 16)

                def early_rows(e):
                    act.wait_ge(e_scl_ready, e + 1)
                    wait_prior(act, e_used, GC * e)
                    nc.scalar.copy(ER[:, 0:GC, D:D + 1].rearrange("p j o -> p (j o)"), e_norm[:, :])
                    for j in range(GC):
                        last = nc.scalar.activation(ER[:, j, 0:D], ER[:, bass.ds(GC * e + j, 1), 0:D].rearrange("p o d -> p (o d)"),
                                                    ACT.Relu, scale=e_scl[:, j:j + 1], bias=e_off[:, j:j + 1])
                    last.then_inc(e_rows, 1)

                def step(i, a):
                    e, late, ahead = look_group(i, a), late_tile(i, a), a < STEPS - 1
                    if done_tile(i, a) is not None:
                        turned_h(i - 2, order(i, a))
                    if late is not None:
                        turned_h(late, order(i, a) + 1)
                        stage(late, order(i, a) + 1, EG, e_added)
                    if sum_group(i, a) is not None:
                        early_rows(sum_group(i, a))
                    if ahead:
                        act.wait_ge(chunk_used, (i - ES) * SPC + GC)
                        hand_idx(i + 1, 0)
                    if e is not None:
                        act.wait_ge(e_var_ready, e + 1)
                        nc.scalar.activation(e_std[:, :], e_var[:, :], ACT.Sqrt).then_inc(e_std_ready, 1)
                    if a == STEPS - 1:
                        turned_h(TILES - 2, TILES - 2)
                    if a - 1 >= ET:
                        stage(i - 1, next_order(i, a), 2 * i + 1 - EG)
                    if ahead:
                        act.wait_ge(chunk_used, (i - ES + 1) * SPC)
                        hand_idx(i + 1, 1)
                    if a + 1 < ES + EG and e is not None:
                        act.wait_ge(looked_up, 2 * (e + 1))
                        load_wide(e + 1)

                load_wide(0)
                hand_idx(ES, 0)
                hand_idx(ES, 1)
                walk(act, step)
                turned_h(TILES - 1, TILES - 1)
                stage(TILES - 1, TILES - 1, GROUPS - EG)
            with act.Else():
                act.wait_ge(all_norm, 1)
                nc.scalar.activation(root[:, :], deg[:, :], ACT.Sqrt).then_inc(all_norm, 1)
                act.wait_ge(all_scaled, 1)
                act.wait_ge(table_done, 16 * BATCHES)
                act.wait_ge(x_again, 32)
                with act.Fori(0, TILES) as t:
                    nc.scalar.activation(H[:, bass.ds(t, 1), 0:D].rearrange("p o d -> p (o d)"),
                                         xall[:, bass.ds(t, 1), :].rearrange("p o d -> p (o d)"), ACT.Relu,
                                         scale=scl[:, bass.ds(t, 1)], bias=off[:, bass.ds(t, 1)]).then_inc(tile_again, 1)
                act.wait_ge(tile_again, TILES)
                act.sem_inc(all_rows)
                with act.Fori(0, GROUPS) as g:
                    act.wait_ge(all_summed, g * TILES + 1)
                    nc.scalar.copy(idx[:, 0:GC], srci[:, bass.ds(g * GC, GC)]).then_inc(idx_ready, 1)
                stage(0, 0, GROUPS * TILES + 1, all_added)
                turned_h(0, 0)
                with act.Fori(1, TILES - 1) as t:
                    stage(t, t, GROUPS * TILES + 1, all_added)
                    turned_h(t, t)
                stage(TILES - 1, TILES - 1, GROUPS * TILES + 1, all_added)
                turned_h(TILES - 1, TILES - 1)

        @block.vector
        def _(dve):
            count = [0]

            def link(ins):
                count[0] += 1
                ins.then_inc(dve_step, 1)
                dve.wait_ge(dve_step, count[0])

            V = nc.vector
            tail = slice(FULL_ROWS // 32 * 32, STEPS)
            V.memset(dst_raw[tail, TAIL_E:STEP_E], N - 1).then_inc(edge_pads, 1)
            V.memset(src_raw[tail, TAIL_E:STEP_E], 0).then_inc(edge_pads, 1)
            dve.wait_ge(early_in, 16)
            V.tensor_copy(early_f, early_raw).then_inc(early_float, 1)
            V.memset(cnt[:, :], 0.0)
            dve.wait_ge(consts, 4)
            V.memset(edge_of_window[:, :], -(WIN - 1.0))
            V.tensor_copy(ident_b[:, :], ident[:, :])
            V.tensor_copy(nodes[:, :], nodes_i[:, :])
            V.tensor_copy(a_first[:, :], a_first_i[:, :]).then_inc(consts_float, 1)
            dve.wait_ge(dst_in, LIST_LOADS)
            V.tensor_single_scalar(b_i, dst_raw, DB - 1, ALU.bitwise_and).then_inc(b_split, 1)
            V.tensor_single_scalar(a_i, dst_raw, 4, ALU.logical_shift_right).then_inc(a_split, 1)

            def statistics(i):
                dve.wait_ge(x_in[i], 16 if i < BATCHES - 1 else 32)
                for t in range(CUTS[i], CUTS[i + 1]):
                    last = V.bn_stats(stats[:, t, :], xall[:, t, :])
                return last

            def variances(i):
                s = slice(*STAT_GROUPS[i])
                V.tensor_tensor(mean2[:, s], stats[:, s, 1], stats[:, s, 4], ALU.add)
                V.tensor_tensor(dif[:, s], stats[:, s, 1], stats[:, s, 4], ALU.subtract)
                link(V.tensor_tensor(var[:, s], stats[:, s, 2], stats[:, s, 5], ALU.add))
                V.tensor_scalar(var[:, s], var[:, s], 1.0 / D, EPS, ALU.mult, ALU.add)
                link(V.scalar_tensor_tensor(out=dif[:, s], in0=dif[:, s], scalar=0.25, in1=dif[:, s],
                                            op0=ALU.mult, op1=ALU.mult))
                V.tensor_tensor(var[:, s], var[:, s], dif[:, s], ALU.add).then_inc(var_ready, 1)

            def scales(i):
                s = slice(*STAT_GROUPS[i])
                dve.wait_ge(std_ready, i + 1)
                link(V.reciprocal(rstd[:, s], std[:, s]))
                V.scalar_tensor_tensor(out=nmr[:, s], in0=mean2[:, s], scalar=-0.5, in1=rstd[:, s],
                                       op0=ALU.mult, op1=ALU.mult).then_inc(ln_ready, 1)

            def hot_digits(n):
                p0, p1 = HOT_PASSES[n]
                if n:
                    dve.wait_ge(counted, p0)
                cs = slice(p0 * PC, p1 * PC)
                m = (p1 - p0) * PC // CB
                for v in range(DB):
                    V.tensor_single_scalar(hot_b[:, 0:m, v, :], digit_b[:, cs].rearrange("p (m c) -> p m c", c=CB), float(v), ALU.is_equal)
                for v in range(DA):
                    last = V.tensor_single_scalar(hot_a[:, 0:m, v, :], digit_a[:, cs].rearrange("p (m c) -> p m c", c=CB), float(v), ALU.is_equal)
                last.then_inc(hot_ready, 1)

            def cut_pass(i):
                q0 = i * (PC // GC) * 4
                dve.wait_ge(counted, i + 1)
                link(V.tensor_tensor(own[:, :, :], banks[4 + i % 2][0:64, 0:PW * CB].rearrange("p (q c) -> p q c", c=CB),
                                     diag[:, :].unsqueeze(1).broadcast_to([64, PW, CB]), ALU.mult))
                link(V.tensor_reduce(part[:, :], own[:, :, :], AX.X, ALU.add))
                if i:
                    dve.wait_ge(cnt_added, i)
                V.tensor_tensor(cnt[:, q0:q0 + PW], cnt[:, q0:q0 + PW], part[:, :], ALU.add).then_inc(cnt_added, 1)

            def degrees(i):
                dve.wait_ge(deg_turned, i + 1)
                s = slice(CUTS[i], CUTS[i + 1])
                V.tensor_single_scalar(deg[:, s], DEG[i % 2][:, s], 1.0, ALU.max).then_inc(deg_ready, 1)

            def norms(i, n, count, rows=True):
                s = slice(CUTS[i], CUTS[i + n])
                dve.wait_ge(root_ready, count)
                link(V.reciprocal(norm[:, s], root[:, s]))
                if rows:
                    V.tensor_tensor(scl[:, s], rstd[:, s], norm[:, s], ALU.mult)
                    V.tensor_tensor(off[:, s], nmr[:, s], norm[:, s], ALU.mult)
                V.tensor_copy(H[:, s, D:ROW], norm[:, s].unsqueeze(2).broadcast_to([P, CUTS[i + n] - CUTS[i], ROW - D])
                              ).then_inc(scale_ready, 1)

            def scale_rows(i, n):
                s = slice(CUTS[i], CUTS[i + 1])
                dve.wait_ge(pre_ready, n)
                V.tensor_tensor(H[:, s, 0:D], H[:, s, 0:D], norm[:, s].unsqueeze(2).broadcast_to([P, CUTS[i + 1] - CUTS[i], D]),
                                ALU.mult).then_inc(dve_rows, 1)

            link(statistics(6))
            dve.wait_ge(consts, 6)
            V.tensor_single_scalar(row_i[:, :], place_i[0:64, :], 2, ALU.logical_shift_right)
            link(V.tensor_single_scalar(lane_b[:, :], place_i[0:64, :], CB - 1, ALU.bitwise_and))
            V.tensor_tensor(diag[:, :], lane_b[:, :].broadcast_to([64, CB]), nodes_i[0:64, 0:CB], ALU.is_equal)
            V.tensor_copy(place[:, :], place_i[:, :])
            dve.wait_ge(early_ready, 1)
            V.tensor_single_scalar(tile_i[:, :], early_idx[:, :], 7, ALU.logical_shift_right).then_inc(early_tiles, 1)
            dve.wait_ge(early_tiles, 1)
            V.tensor_copy(tile_f[:, :], tile_i[:, :])
            V.memset(pick[:, :], 0.0)
            V.tensor_scalar(step_node[:, :], nodes[:, 0:STEPS], float(NPC * SPC), -float(BACK), ALU.mult, ALU.add)
            link(V.tensor_single_scalar(chunk_node[:, :], nodes[:, 0:SPC], float(NPC), ALU.mult))
            V.tensor_tensor(pick[:, P - DB:P], row_i[:, :].broadcast_to([64, DB]), nodes_i[0:64, 0:DB], ALU.is_equal)
            link(V.tensor_tensor(first[:, :].rearrange("p (s j) -> p s j", j=SPC),
                                 step_node[:, :].unsqueeze(2).broadcast_to([P, STEPS, SPC]),
                                 chunk_node[:, :].unsqueeze(1).broadcast_to([P, STEPS, SPC]), ALU.add))
            dve.wait_ge(digits_ready, 1)
            V.memset(digit_a[P // 2:P, REAL_CH - 1:REAL_CH], float(DA))
            link(V.memset(digit_a[:, REAL_CH:CH], float(DA)))
            hot_digits(0)
            rel_v = rel[:, :].rearrange("p (s j) -> p j s", j=SPC)
            first_v = first[:, :].rearrange("p (s j) -> p j s", j=SPC)
            for k in range(4):
                dve.wait_ge(dst_turned, k + 1)
                last = V.tensor_tensor(rel_v[:, 4 * k:4 * k + 4, :],
                                       banks[4 + k][:, 0:4 * STEPS].rearrange("p (j s) -> p j s", j=4),
                                       first_v[:, 4 * k:4 * k + 4, :], ALU.subtract)
            last.then_inc(rel_ready, 1)
            link(statistics(5))
            variances(0)
            scales(0)
            statistics(0)
            link(statistics(1))
            variances(1)
            cut_pass(0)
            cut_pass(1)
            hot_digits(1)
            scales(1)
            degrees(0)
            degrees(1)
            statistics(2)
            norms(0, 2, 1)
            link(statistics(3))
            variances(2)
            cut_pass(2)
            cut_pass(3)
            hot_digits(2)
            scales(2)
            degrees(2)
            degrees(3)
            link(statistics(4))
            variances(3)
            norms(2, 2, 2)
            dve.wait_ge(outside_ready, 1)
            link(V.tensor_tensor(outside[:, 2:3], outside[:, 0:1], outside[:, 1:2], ALU.add))
            V.memset(rel[P // 2:P, REAL_CH - 1:REAL_CH], FAR)
            V.memset(rel[:, REAL_CH:CH], FAR).then_inc(outside_summed, 1)
            scales(3)
            cut_pass(4)
            cut_pass(5)
            dve.wait_ge(outside_turned, 1)
            link(V.tensor_reduce(flag[0:1, 0:1], banks[6][0:1, 0:P], AX.X, ALU.max))
            V.tensor_single_scalar(flag_i[0:1, 0:1], flag[0:1, 0:1], 0.5, ALU.is_lt).then_inc(flag_ready, 1)
            hot_digits(3)
            degrees(4)
            degrees(5)
            norms(4, 2, 3)
            dve.wait_ge(scale_ready, 3)
            scale_rows(5, 2)
            cut_pass(6)
            degrees(6)
            norms(6, 1, 4, False)
            dve.wait_ge(scale_ready, 4)
            scale_rows(6, 1)

            quick = flag_value(dve)
            with dve.If(quick == 0):
                dve.sem_inc(own_general)
                V.tensor_tensor(n_i, rel[:, :], first[:, :], ALU.add).then_inc(own_general, 1)
                dve.wait_ge(own_general, 2)
                V.tensor_single_scalar(lo_i, n_i, P - 1, ALU.bitwise_and)
                V.tensor_single_scalar(hi_i, n_i, 7, ALU.arith_shift_right).then_inc(own_general, 1)
                dve.wait_ge(own_general, 3)
                V.tensor_copy(lo_f, lo_i)
                V.tensor_copy(hi_f, hi_i).then_inc(own_general, 1)
                dve.wait_ge(own_general, 4)
                with dve.Fori(0, GROUPS) as g:
                    dve.wait_ge(all_counted, g + 1)
                    for j in range(GC):
                        V.tensor_scalar(hot_lo[:, j, :], nodes[:, :], lo_f[:, bass.ds(g * GC + j, 1)], None, ALU.is_equal)
                        last = V.tensor_scalar(hot_hi[:, j, :], nodes[:, :], hi_f[:, bass.ds(g * GC + j, 1)], None, ALU.is_equal)
                    last.then_inc(all_hot_ready, 1)
                dve.wait_ge(all_counted, GROUPS + 1)
                V.tensor_copy(deg_sb[0:TILES, :], banks[4][0:TILES, 0:P]).then_inc(rows_counted, 1)
                dve.wait_ge(deg_turned, PASSES + 1)
                V.tensor_single_scalar(deg[:, :], banks[7][:, 0:TILES], 1.0, ALU.max).then_inc(all_norm, 1)
                dve.wait_ge(all_norm, 2)
                V.reciprocal(norm[:, :], root[:, :]).then_inc(all_norm, 1)
                dve.wait_ge(all_norm, 3)
                dve.wait_ge(table_done, 16 * BATCHES)
                V.tensor_tensor(scl[:, :], rstd[:, :], norm[:, :], ALU.mult)
                V.tensor_tensor(off[:, :], nmr[:, :], norm[:, :], ALU.mult)
                V.tensor_copy(H[:, :, D:ROW], norm[:, :].unsqueeze(2).broadcast_to([P, TILES, ROW - D])).then_inc(all_scaled, 1)

            V.tensor_copy(NODES[:, 0:WIN], nodes[:, :]).then_inc(bank_nodes, 1)
            dve.wait_ge(bank_nodes, 1)

            def finish(t, n):
                r = rows_of(t)
                x_t, o_t = (x_last, o_last) if is_last(t) else (x_st, o_st)
                dve.wait_ge(fin_mm, n + 1)
                if is_last(t):
                    dve.wait_ge(x_last_in, 16)
                else:
                    dve.wait_ge(x_loaded, 16 * (n + 1))
                V.scalar_tensor_tensor(out=t1[0:r, :], in0=SELF[0:r, 0:D], scalar=FIN[0:r, D:D + 1], in1=x_t[0:r, :],
                                       op0=ALU.mult, op1=ALU.add).then_inc(t1_done, 1)
                dve.wait_ge(t1_done, n + 1)
                if not is_last(t):
                    wait_prior(dve, stored, 16 * n)
                V.scalar_tensor_tensor(out=o_t[0:r, :], in0=FIN[0:r, 0:D], scalar=norm[0:r, bass.ds(t, 1)],
                                       in1=t1[0:r, :], op0=ALU.mult, op1=ALU.add).then_inc(out_ready, 1)

            with dve.If(quick == 1):
                clear = EG * NPC * GC + PAD - BACK + GW - NPC * GC
                dve.wait_ge(table_done, 16 * BATCHES)
                V.memset(AG[:, 0:clear], 0.0)
                V.memset(SR[SP_ROW:SP_ROW + 1, 0:clear], 0.0).then_inc(sums_clear, 1)
                dve.wait_ge(sums_clear, 1)

                def hots(i, half, k, prior):
                    for j in range(half * GC, half * GC + k):
                        if prior and j % 4 == 0:
                            dve.wait_ge(chunk_used, (i - ES - 1) * SPC + j + 4)
                        V.tensor_scalar(OH[:, j, :], NODES[:, 0:WIN], rel[:, bass.ds(i * SPC + j, 1)], None,
                                        ALU.is_equal).then_inc(hot, 1)

                def add(g, half, k=GC, prior=True):
                    w = WIN + NPC * (k - 1)
                    at = g * (NPC * GC) + PAD - BACK
                    dve.wait_ge(chunk_used, (g - EG) * GC + k)
                    if prior:
                        dve.wait_ge(group_added, g - EG)
                    old = min(GW - NPC * GC, w)
                    for sums, ps in ((AG[:, :], agg_ps[half][:, :]),
                                     (SR[SP_ROW:SP_ROW + 1, :], s_ps[half][SP_ROW:SP_ROW + 1, :])):
                        last = V.tensor_tensor(sums[:, bass.ds(at, old)], sums[:, bass.ds(at, old)], ps[:, 0:old], ALU.add)
                        if w > old:
                            last = V.tensor_copy(sums[:, bass.ds(at + old, w - old)], ps[:, old:w])
                    last.then_inc(group_added, 1)

                LINKS = 7

                def mine(ins, e, c):
                    ins.then_inc(early_step, 1)
                    dve.wait_ge(early_step, e * LINKS + c)

                def early_places(e):
                    dve.wait_ge(wide_in, 16 * (e + 1))
                    mine(V.tensor_single_scalar(wide, wide, P - 1, ALU.bitwise_and), e, 1)
                    V.tensor_scalar(at_place, wide, place[:, 0:1], None, ALU.is_equal).then_inc(place_ready, 1)

                def early_variances(e):
                    for j in range(GC):
                        last = V.bn_stats(e_stats[:, j, :], ER[:, bass.ds(GC * e + j, 1), 0:D].rearrange("p o d -> p (o d)"))
                    mine(last, e, 2)
                    V.tensor_tensor(e_mean2[:, :], e_stats[:, :, 1], e_stats[:, :, 4], ALU.add)
                    V.tensor_tensor(e_dif[:, :], e_stats[:, :, 1], e_stats[:, :, 4], ALU.subtract)
                    mine(V.tensor_tensor(e_var[:, :], e_stats[:, :, 2], e_stats[:, :, 5], ALU.add), e, 3)
                    V.tensor_scalar(e_var[:, :], e_var[:, :], 1.0 / D, EPS, ALU.mult, ALU.add)
                    mine(V.scalar_tensor_tensor(out=e_dif[:, :], in0=e_dif[:, :], scalar=0.25, in1=e_dif[:, :],
                                                op0=ALU.mult, op1=ALU.mult), e, 4)
                    V.tensor_tensor(e_var[:, :], e_var[:, :], e_dif[:, :], ALU.add).then_inc(e_var_ready, 1)

                def early_norms(e, half):
                    dve.wait_ge(looked_up, 2 * e + half + 1)
                    for j in range(GC // 2):
                        last = V.scalar_tensor_tensor(out=found[:, j, :], in0=nodes[:, 0:TILES],
                                                      scalar=tile_f[:, bass.ds(GC * e + half * (GC // 2) + j, 1)],
                                                      in1=LOOK[:, j * TILES:(j + 1) * TILES], op0=ALU.is_equal, op1=ALU.mult)
                    last.then_inc(picked, 1)
                    dve.wait_ge(picked, 2 * e + half + 1)
                    if half == 0:
                        wait_prior(dve, e_rows, e)
                    mine(V.tensor_reduce(e_norm[:, half * (GC // 2):(half + 1) * (GC // 2)], found[:, :, :], AX.X, ALU.add),
                         e, 5 + half)

                def early_scales(e):
                    dve.wait_ge(e_std_ready, e + 1)
                    mine(V.reciprocal(e_rstd[:, :], e_std[:, :]), e, 7)
                    V.tensor_tensor(e_scl[:, :], e_rstd[:, :], e_norm[:, :], ALU.mult).then_inc(e_scaled, 1)
                    dve.wait_ge(e_scaled, e + 1)
                    V.scalar_tensor_tensor(out=e_off[:, :], in0=e_mean2[:, :], scalar=-0.5, in1=e_scl[:, :],
                                           op0=ALU.mult, op1=ALU.mult).then_inc(e_scl_ready, 1)

                def early_hots(e):
                    wait_prior(dve, e_used, GC * e)
                    V.tensor_tensor(early_oh[:, :, :], NODES[:, 0:WIN].unsqueeze(1).broadcast_to([P, GC, WIN]),
                                    rel[:, bass.ds(GC * e, GC)].unsqueeze(2).broadcast_to([P, GC, WIN]),
                                    ALU.is_equal).then_inc(e_hot, 1)

                def early_add(e):
                    at = e * (NPC * GC) + PAD - BACK
                    dve.wait_ge(e_used, GC * (e + 1))
                    dve.wait_ge(group_added, 2)
                    wait_prior(dve, e_added, e)
                    V.tensor_tensor(AG[:, bass.ds(at, GW)], AG[:, bass.ds(at, GW)], SUM_E[:, 0:GW], ALU.add)
                    V.tensor_tensor(SR[SP_ROW:SP_ROW + 1, bass.ds(at, GW)], SR[SP_ROW:SP_ROW + 1, bass.ds(at, GW)],
                                    s_ps[2][SP_ROW:SP_ROW + 1, 0:GW], ALU.add).then_inc(e_added, 1)

                def step(i, a):
                    k, prior = LAST_CH if a == STEPS - 1 else SPC, a > ES
                    e, late = look_group(i, a), late_tile(i, a)
                    hots(i, 0, min(k, GC), prior)
                    if prior:
                        add(2 * i - 1, 1, GC, True)
                    if add_group(i, a) is not None:
                        early_add(add_group(i, a))
                    if sum_group(i, a) is not None:
                        early_hots(sum_group(i, a))
                    if e is not None:
                        early_places(e)
                        if a == ES:
                            dve.wait_ge(early_landed, 16 * EC)
                        early_variances(e)
                    hots(i, 1, k - GC, prior)
                    if done_tile(i, a) is not None:
                        finish(i - 2, order(i, a))
                    if e is not None:
                        early_norms(e, 0)
                    if late is not None:
                        finish(late, order(i, a) + 1)
                    add(2 * i, 0, GC, prior)
                    if e is not None:
                        early_norms(e, 1)
                        early_scales(e)

                walk(dve, step)
                add(GROUPS - 1, 1, LAST_CH - GC)
                finish(TILES - 2, TILES - 2)
                finish(TILES - 1, TILES - 1)
            with dve.Else():
                dve.wait_ge(sums_clear, 2)
                for primed in (all_hot, all_added, grel_ready):
                    dve.sem_inc(primed)
                with dve.Fori(0, GROUPS) as g:
                    dve.wait_ge(all_hot, g * TILES + 1)
                    dve.wait_ge(grel_ready, g * (TILES + 1) + 1)
                    V.tensor_tensor(grel[:, :], rel[:, bass.ds(g * GC, GC)], first[:, bass.ds(g * GC, GC)],
                                    ALU.add).then_inc(grel_ready, 1)
                    with dve.Fori(0, TILES) as w:
                        visit = g * TILES + w
                        dve.wait_ge(grel_ready, visit + g + 2)
                        dve.wait_ge(all_summed, visit + 1)
                        for j in range(GC):
                            last = V.tensor_scalar(OH[:, j, :], nodes[:, :], grel[:, j:j + 1], None, ALU.is_equal)
                        last.then_inc(all_hot, 1)
                        dve.wait_ge(all_hot, visit + 2)
                        V.tensor_single_scalar(grel[:, :], grel[:, :], -float(P), ALU.add).then_inc(grel_ready, 1)
                        dve.wait_ge(all_summed, visit + 2)
                        dve.wait_ge(all_added, visit + 1)
                        at = w * P + PAD
                        V.tensor_tensor(AG[:, bass.ds(at, P)], AG[:, bass.ds(at, P)], SUM_A[:, 0:P], ALU.add)
                        V.tensor_tensor(SR[SP_ROW:SP_ROW + 1, bass.ds(at, P)], SR[SP_ROW:SP_ROW + 1, bass.ds(at, P)],
                                        s_ps[0][SP_ROW:SP_ROW + 1, 0:P], ALU.add).then_inc(all_added, 1)
                finish(0, 0)
                with dve.Fori(1, TILES - 1) as t:
                    finish(t, t)
                finish(TILES - 1, TILES - 1)

        @block.tensor
        def _(pe):
            T = nc.tensor
            pe.wait_ge(consts, 1)
            pe.wait_ge(early_float, 1)
            T.transpose(banks[7][:, 0:EC], early_f, ident[0:EC, 0:EC]).then_inc(early_turned, 1)
            for k in range(2 * SPC):
                raw = (b_raw, a_raw)[k // SPC]
                if k % SPC == 0:
                    pe.wait_ge(digits_float, k // SPC + 1)
                j = k % 8
                last = T.transpose(banks[k // 8][:, :].bitcast(bf16)[:, j * STEPS:(j + 1) * STEPS],
                                   raw[:, (k % SPC) * P:(k % SPC + 1) * P], ident_b[0:STEPS, 0:STEPS])
                if j == 7:
                    last.then_inc(digits_turned, 1)
            pe.wait_ge(dst_float, 1)
            pe.wait_ge(early_ready, 1)
            for k in range(SPC):
                last = T.transpose(banks[4 + k // 4][:, (k % 4) * STEPS:(k % 4 + 1) * STEPS], dst_f[:, k * P:(k + 1) * P],
                                   ident[0:STEPS, 0:STEPS])
                if k % 4 == 3:
                    last.then_inc(dst_turned, 1)

            def count_passes(n):
                pe.wait_ge(hot_ready, n + 1)
                for i in range(*HOT_PASSES[n]):
                    m0 = (i - HOT_PASSES[n][0]) * PC // CB
                    for m in range(PC // CB):
                        q0 = (m * CB // GC) * 4
                        last = T.matmul(banks[4 + i % 2][0:64, q0 * CB:(q0 + DA) * CB],
                                        hot_b[:, m0 + m].rearrange("p v c -> p (v c)"),
                                        hot_a[:, m0 + m].rearrange("p v c -> p (v c)"),
                                        start=(m == 0), stop=(m == PC // CB - 1), skip_group_check=True)
                    last.then_inc(counted, 1)

            def turn_counts(i):
                t0, t1 = CUTS[i], CUTS[i + 1]
                pe.wait_ge(cnt_added, i + 1)
                if i == 1:
                    pe.wait_ge(src_ready, 1)
                if i > 1:
                    pe.wait_ge(deg_ready, i - 1)
                for a in range(TQ):
                    q0 = PAD // DB + t0 * TQ + a
                    last = T.matmul(DEG[i % 2][:, t0:t1], pick[:, P - DB - DB * a:2 * P - DB - DB * a],
                                    cnt[:, q0:q0 + (t1 - t0 - 1) * TQ + 1:TQ],
                                    start=(a == 0), stop=(a == TQ - 1), skip_group_check=True)
                last.then_inc(deg_turned, 1)

            pe.wait_ge(digits_ready, 1)
            pe.wait_ge(src_float, 1)
            for k in range(SPC):
                last = T.transpose(banks[k // 4][:, (k % 4) * STEPS:(k % 4 + 1) * STEPS],
                                   src_f[:, k * P:(k + 1) * P], ident[0:STEPS, 0:STEPS])
                if k % 4 == 3:
                    last.then_inc(src_turned, 1)
            pe.wait_ge(rel_ready, 1)
            count_passes(0)
            turn_counts(0)
            turn_counts(1)
            count_passes(1)
            turn_counts(2)
            turn_counts(3)
            count_passes(2)
            pe.wait_ge(outside_summed, 1)
            T.transpose(banks[6][0:1, 0:P], outside[:, 2:3], ident[:, :]).then_inc(outside_turned, 1)
            turn_counts(4)
            turn_counts(5)
            pe.wait_ge(flag_ready, 1)
            pe.wait_ge(w_loaded, 32)
            for k in range(2):
                last = T.transpose(banks[6][:, k * D:(k + 1) * D], w_in[:, k * D:(k + 1) * D], ident[:, :])
            last.then_inc(w_turned, 1)
            count_passes(3)
            turn_counts(6)

            quick = flag_value(pe)
            with pe.If(quick == 0):
                pe.sem_inc(all_counted)

                def count_group(g, start):
                    pe.wait_ge(all_hot_ready, g + 1)
                    for j in range(GC):
                        last = T.matmul(banks[4][:, 0:P], hot_hi[:, j, :], hot_lo[:, j, :],
                                        start=start and j == 0, stop=False, skip_group_check=True)
                    last.then_inc(all_counted, 1)

                count_group(0, True)
                with pe.Fori(1, GROUPS) as g:
                    count_group(g, False)
                pe.wait_ge(rows_counted, 1)
                T.transpose(banks[7][:, 0:TILES], deg_sb[0:TILES, :], ident[0:TILES, 0:TILES]).then_inc(deg_turned, 1)

            def turn_tile(t, n):
                r = rows_of(t)
                pe.wait_ge(h_loaded, 16 * (n + 1))
                T.transpose(TURN[:, 0:r], h_st[0:r, 0:D], ident[0:r, 0:r]).then_inc(h_turned, 1)

            def finish_tile(t, n):
                r = rows_of(t)
                pe.wait_ge(hT_ready, n + 1)
                pe.wait_ge(staged, n + 1)
                wait_prior(pe, out_ready, n)
                T.matmul(SELF[0:r, 0:D], hT[:, 0:r], wT[:, 0:D], start=True, stop=True)
                T.matmul(FIN[0:r, 0:D + 1], s_st[0:1, 0:r], brow[0:1, :], start=True, stop=False, skip_group_check=True)
                T.matmul(FIN[0:r, 0:D], a_st[:, 0:r], wT[:, D:2 * D], start=False, stop=True,
                         skip_group_check=True).then_inc(fin_mm, 1)

            def sum_chunk(agg, s_out, j, start, stop, rows=G, onehot=OH):
                T.matmul(agg, rows[:, j, 0:D], onehot[:, j, :], start=start, stop=stop, skip_group_check=True)
                return T.matmul(s_out, rows[:, j, D - SP_ROW:D + 1], onehot[:, j, :], start=False, stop=stop, skip_group_check=True)

            pe.wait_ge(w_ready, 1)
            with pe.If(quick == 1):
                def look_up(e, half):
                    pe.wait_ge(place_ready, e + 1)
                    wait_prior(pe, picked, 2 * e + half)
                    for j in range(GC // 2):
                        c = half * (GC // 2) + j
                        last = T.matmul(LOOK[:, j * TILES:(j + 1) * TILES], at_place[:, c * P:(c + 1) * P], norm[:, :],
                                        start=(j == 0), stop=(j == GC // 2 - 1), skip_group_check=True)
                    last.then_inc(looked_up, 1)

                def early_sum(e, jj):
                    if jj == 0:
                        pe.wait_ge(e_rows, e + 1)
                        pe.wait_ge(e_hot, e + 1)
                        wait_prior(pe, e_added, e)
                    c0 = NPC * jj
                    sum_chunk(SUM_E[:, c0:c0 + WIN], s_ps[2][0:SP_ROW + 1, c0:c0 + WIN], jj, jj == 0, jj == GC - 1,
                              ER, early_oh).then_inc(e_used, 1)

                def step(i, a):
                    k = LAST_CH if a == STEPS - 1 else SPC
                    late, n = late_tile(i, a), order(i, a)
                    for j in range(k):
                        half, jj = j // GC, j % GC
                        if jj == 0 and a > ES:
                            pe.wait_ge(group_added, 2 * (i - ES) - 1 + half)
                        pe.wait_ge(landed[j], 16 * (i - ES + 1))
                        pe.wait_ge(hot, (i - ES) * SPC + j + 1)
                        c0 = NPC * jj
                        stop = jj == GC - 1 or j == k - 1
                        last = sum_chunk(agg_ps[half][:, c0:c0 + WIN],
                                         s_ps[half][0:SP_ROW + 1, c0:c0 + WIN], j, jj == 0, stop)
                        last.then_inc(chunk_used, 1)
                        if j == 0 and done_tile(i, a) is not None:
                            turn_tile(i - 2, n)
                        if j == 3 and done_tile(i, a) is not None:
                            finish_tile(i - 2, n)
                        if late is not None and j == 4:
                            turn_tile(late, n + 1)
                        if late is not None and j == 6:
                            finish_tile(late, n + 1)
                        if a == STEPS - 1 and j == k - 3:
                            turn_tile(TILES - 2, TILES - 2)
                        if look_group(i, a) is not None and j in (5, 11):
                            look_up(look_group(i, a), j // GC)
                        if sum_group(i, a) is not None and j >= GC:
                            early_sum(sum_group(i, a), jj)

                walk(pe, step)
                finish_tile(TILES - 2, TILES - 2)
                turn_tile(TILES - 1, TILES - 1)
                finish_tile(TILES - 1, TILES - 1)
            with pe.Else():
                pe.sem_inc(all_summed)
                with pe.Fori(0, GROUPS) as g:
                    for j in range(GC):
                        pe.wait_ge(landed[j], 16 * (g + 1))
                    pe.sem_inc(waited)
                    with pe.Fori(0, TILES) as w:
                        visit = g * TILES + w
                        pe.wait_ge(all_added, visit + 1)
                        pe.wait_ge(all_hot, visit + 2)
                        for j in range(GC):
                            last = sum_chunk(SUM_A[:, 0:P], s_ps[0][0:SP_ROW + 1, 0:P], j, j == 0, j == GC - 1)
                        last.then_inc(all_summed, 1)
                turn_tile(0, 0)
                finish_tile(0, 0)
                with pe.Fori(1, TILES - 1) as t:
                    turn_tile(t, t)
                    finish_tile(t, t)
                turn_tile(TILES - 1, TILES - 1)
                finish_tile(TILES - 1, TILES - 1)


def kernel(x, src, dst, L0_gnn_W, L0_gnn_b):
    import numpy as np
    import concourse.bacc as bacc
    from concourse.bass_utils import run_bass_kernel_spmd

    nc = bacc.Bacc("TRN2", target_bir_lowering=False, num_devices=1)
    arrays, args = {}, []
    for name, a in (("x", x), ("src", src), ("dst", dst), ("W", L0_gnn_W), ("b", L0_gnn_b)):
        a = np.ascontiguousarray(a)
        arrays[f"in_{name}"] = a
        args.append(nc.dram_tensor(f"in_{name}", a.shape, mybir.dt.from_np(a.dtype), kind="ExternalInput").ap())
    out = nc.dram_tensor("out_nodes", args[0].shape, mybir.dt.float32, kind="ExternalOutput").ap()
    gnn_layer(nc, *args, out)
    r = run_bass_kernel_spmd(nc, [arrays], core_ids=[0])
    return r.results[0]["out_nodes"]
```
